# Optimizing a Trainium2 kernel written in Bass

```python
import numpy as np
import jax
import jax.numpy as jnp

def _softmax(x, axis=-1):
    return jax.nn.softmax(x, axis=axis)

def _gelu(x):
    return jax.nn.gelu(x, approximate=True)

def _silu(x):
    return jax.nn.silu(x)

def _sigmoid(x):
    return jax.nn.sigmoid(x)

def _layernorm(x, axis=-1, eps=1e-05):
    m = jnp.mean(x, axis=axis, keepdims=True)
    v = jnp.var(x, axis=axis, keepdims=True)
    return (x - m) / jnp.sqrt(v + eps)

def _scatter_add(tgt, idx, src, axis=0):
    return tgt.at[idx].add(src)

def _segment_sum(src, seg, n):
    return jax.ops.segment_sum(src, seg, n)
kernel_name = 'mk_prb_d2_jaxref_r8_cd10b5'

def setup_inputs(seed: int=0):
    np.random.seed(seed)
    _w = jnp.asarray

    def _L0_attn_setup():
        import jax, jax.numpy as jnp
        import numpy as np
        EPS = 1e-15
        HEAD_DIM = 32
        PAD_VAL = 1.0
        key = jax.random.key(seed)
        k1, k2, k3, k4 = jax.random.split(key, 4)
        B, N, C = (2, 512, 256)
        s = 1.0 / np.sqrt(C).astype(np.float32)
        x = jax.random.normal(k1, (B, N, C), jnp.float32)
        w_qkv = jax.random.normal(k2, (3 * C, C), jnp.float32) * s
        w_proj = jax.random.normal(k3, (C, C), jnp.float32) * s
        b_proj = jax.random.normal(k4, (C,), jnp.float32) * 0.01
        return {'x': x, 'w_qkv': w_qkv, 'w_proj': w_proj, 'b_proj': b_proj}
    _L0_attn_in = _L0_attn_setup()

    def _L0_ffn_setup():
        import jax, jax.numpy as jnp
        import numpy as np
        B, S, D = (2, 256, 256)
        MOE_D = 176
        E = 16
        K = 6
        ALPHA = 0.001

        def _moe_forward(x, gate_w, w_gate, w_up, w_down):
            b, s, d = x.shape
            T = b * s
            h = x.reshape(T, d)
            logits = h @ gate_w.T
            scores = jax.nn.softmax(logits.astype(jnp.float32), axis=-1)
            topk_w, topk_idx = jax.lax.top_k(scores, K)
            cw = jnp.zeros((T, E), jnp.float32)
            cw = cw.at[jnp.arange(T)[:, None], topk_idx].add(topk_w)
            y = jnp.zeros((T, d), x.dtype)
            for e in range(E):
                g = h @ w_gate[e].T
                u = h @ w_up[e].T
                out = jax.nn.silu(g) * u @ w_down[e].T
                y = y + cw[:, e:e + 1].astype(x.dtype) * out
            counts = jnp.sum(jax.nn.one_hot(topk_idx.reshape(b, s * K), E, dtype=jnp.float32), axis=1)
            ce = counts * (E / (s * K))
            scores_bse = scores.reshape(b, s, E)
            aux = jnp.mean(jnp.sum(ce * scores_bse.mean(axis=1), axis=1)) * ALPHA
            return (y.reshape(b, s, d), aux)
        key = jax.random.key(seed)
        ks = jax.random.split(key, 5)
        sd = 1.0 / np.sqrt(D)
        sm = 1.0 / np.sqrt(MOE_D)
        return {'x': jax.random.normal(ks[0], (B, S, D), jnp.float32), 'gate_w': jax.random.normal(ks[1], (E, D), jnp.float32) * sd, 'w_gate': jax.random.normal(ks[2], (E, MOE_D, D), jnp.float32) * sd, 'w_up': jax.random.normal(ks[3], (E, MOE_D, D), jnp.float32) * sd, 'w_down': jax.random.normal(ks[4], (E, D, MOE_D), jnp.float32) * sm}
    _L0_ffn_in = _L0_ffn_setup()

    def _L1_attn_setup():
        import jax, jax.numpy as jnp
        import numpy as np
        DIM = 256
        HIDDEN = 512
        BATCH = 4
        SEQ = 256
        key = jax.random.key(seed)
        ks = jax.random.split(key, 4)
        scale_in = 1.0 / np.sqrt(DIM)
        scale_out = 1.0 / np.sqrt(HIDDEN)
        return {'x': jax.random.normal(ks[0], (BATCH, SEQ, DIM), dtype=jnp.float32), 'W_in': jax.random.normal(ks[1], (HIDDEN, DIM), dtype=jnp.float32) * scale_in, 'b_in': jnp.zeros((HIDDEN,), dtype=jnp.float32), 'W_out': jax.random.normal(ks[2], (DIM, HIDDEN), dtype=jnp.float32) * scale_out, 'b_out': jnp.zeros((DIM,), dtype=jnp.float32), 'gamma': jnp.ones((HIDDEN,), dtype=jnp.float32), 'beta': jnp.zeros((HIDDEN,), dtype=jnp.float32)}
    _L1_attn_in = _L1_attn_setup()

    def _L1_ffn_setup():
        import jax, jax.numpy as jnp
        import numpy as np
        B, S, H = (2, 128, 256)
        E, K, F = (8, 2, 176)
        N_SHARED = 2
        FS = F * N_SHARED
        ROUTED_SCALE = 1.0

        def _swiglu_mlp(x, wg, wu, wd):
            return jax.nn.silu(x @ wg.T) * (x @ wu.T) @ wd.T
        key = jax.random.key(seed)
        ks = jax.random.split(key, 8)

        def w(k, shape, fan_in):
            return jax.random.normal(k, shape, jnp.float32) * (1.0 / np.sqrt(fan_in))
        return {'hidden_states': jax.random.normal(ks[0], (B, S, H), jnp.float32), 'gate_weight': w(ks[1], (E, H), H), 'w_gate': w(ks[2], (E, F, H), H), 'w_up': w(ks[3], (E, F, H), H), 'w_down': w(ks[4], (E, H, F), F), 'sw_gate': w(ks[5], (FS, H), H), 'sw_up': w(ks[6], (FS, H), H), 'sw_down': w(ks[7], (H, FS), FS)}
    _L1_ffn_in = _L1_ffn_setup()
    _d = {'L0_attn_x': _L0_attn_in['x'], 'L0_attn_w_qkv': _L0_attn_in['w_qkv'], 'L0_attn_w_proj': _L0_attn_in['w_proj'], 'L0_attn_b_proj': _L0_attn_in['b_proj'], 'L0_ffn_gate_w': _L0_ffn_in['gate_w'], 'L0_ffn_w_gate': _L0_ffn_in['w_gate'], 'L0_ffn_w_up': _L0_ffn_in['w_up'], 'L0_ffn_w_down': _L0_ffn_in['w_down'], 'L1_attn_W_in': _L1_attn_in['W_in'], 'L1_attn_b_in': _L1_attn_in['b_in'], 'L1_attn_W_out': _L1_attn_in['W_out'], 'L1_attn_b_out': _L1_attn_in['b_out'], 'L1_attn_gamma': _L1_attn_in['gamma'], 'L1_attn_beta': _L1_attn_in['beta'], 'L1_ffn_gate_weight': _L1_ffn_in['gate_weight'], 'L1_ffn_w_gate': _L1_ffn_in['w_gate'], 'L1_ffn_w_up': _L1_ffn_in['w_up'], 'L1_ffn_w_down': _L1_ffn_in['w_down'], 'L1_ffn_sw_gate': _L1_ffn_in['sw_gate'], 'L1_ffn_sw_up': _L1_ffn_in['sw_up'], 'L1_ffn_sw_down': _L1_ffn_in['sw_down']}
    _x0 = _d['L0_attn_x']
    _d['L0_attn_x'] = jax.random.normal(jax.random.fold_in(jax.random.key(seed), 1), (4, 512, 256), dtype=_x0.dtype)
    del _x0
    return _d

def reference(L0_attn_x, L0_attn_w_qkv, L0_attn_w_proj, L0_attn_b_proj, L0_ffn_gate_w, L0_ffn_w_gate, L0_ffn_w_up, L0_ffn_w_down, L1_attn_W_in, L1_attn_b_in, L1_attn_W_out, L1_attn_b_out, L1_attn_gamma, L1_attn_beta, L1_ffn_gate_weight, L1_ffn_w_gate, L1_ffn_w_up, L1_ffn_w_down, L1_ffn_sw_gate, L1_ffn_sw_up, L1_ffn_sw_down):

    def _L0_attn_ref(x, w_qkv, w_proj, b_proj):
        import jax, jax.numpy as jnp
        import numpy as np
        EPS = 1e-15
        HEAD_DIM = 32
        PAD_VAL = 1.0
        B, N, C = x.shape
        d = HEAD_DIM
        h = C // d
        qkv = (x @ w_qkv.T).reshape(B, N, 3, C)
        q, k, v = (qkv[:, :, 0], qkv[:, :, 1], qkv[:, :, 2])

        def to_heads(t):
            return t.reshape(B, N, h, d).transpose(0, 2, 3, 1)
        q = jax.nn.relu(to_heads(q))
        k = jax.nn.relu(to_heads(k))
        v = to_heads(v)
        v_pad = jnp.pad(v, ((0, 0), (0, 0), (0, 1), (0, 0)), constant_values=PAD_VAL)
        vk = jnp.einsum('bhen,bhdn->bhed', v_pad, k)
        out = jnp.einsum('bhed,bhdn->bhen', vk, q)
        out = out[:, :, :-1] / (out[:, :, -1:] + EPS)
        out = out.reshape(B, C, N).transpose(0, 2, 1)
        return out @ w_proj.T + b_proj

    def _L0_ffn_ref(x, gate_w, w_gate, w_up, w_down):
        import jax, jax.numpy as jnp
        import numpy as np
        B, S, D = (2, 256, 256)
        MOE_D = 176
        E = 16
        K = 6
        ALPHA = 0.001

        def _moe_forward(x, gate_w, w_gate, w_up, w_down):
            b, s, d = x.shape
            T = b * s
            h = x.reshape(T, d)
            logits = h @ gate_w.T
            scores = jax.nn.softmax(logits.astype(jnp.float32), axis=-1)
            topk_w, topk_idx = jax.lax.top_k(scores, K)
            cw = jnp.zeros((T, E), jnp.float32)
            cw = cw.at[jnp.arange(T)[:, None], topk_idx].add(topk_w)
            y = jnp.zeros((T, d), x.dtype)
            for e in range(E):
                g = h @ w_gate[e].T
                u = h @ w_up[e].T
                out = jax.nn.silu(g) * u @ w_down[e].T
                y = y + cw[:, e:e + 1].astype(x.dtype) * out
            counts = jnp.sum(jax.nn.one_hot(topk_idx.reshape(b, s * K), E, dtype=jnp.float32), axis=1)
            ce = counts * (E / (s * K))
            scores_bse = scores.reshape(b, s, E)
            aux = jnp.mean(jnp.sum(ce * scores_bse.mean(axis=1), axis=1)) * ALPHA
            return (y.reshape(b, s, d), aux)
        y, _aux = _moe_forward(x, gate_w, w_gate, w_up, w_down)
        return y

    def _L1_attn_ref(x, W_in, b_in, W_out, b_out, gamma, beta):
        import jax, jax.numpy as jnp
        import numpy as np
        DIM = 256
        HIDDEN = 512
        BATCH = 4
        SEQ = 256
        u = jnp.einsum('bsd,hd->bsh', x, W_in) + b_in

        def step(state, u_t):
            s = jnp.tanh(u_t + state * gamma + beta)
            return (s, s)
        init = jnp.zeros((x.shape[0], W_in.shape[0]), dtype=x.dtype)
        _, states = jax.lax.scan(step, init, jnp.swapaxes(u, 0, 1))
        states = jnp.swapaxes(states, 0, 1)
        y = jnp.einsum('bsh,dh->bsd', states, W_out) + b_out
        return y

    def _L1_ffn_ref(hidden_states, gate_weight, w_gate, w_up, w_down, sw_gate, sw_up, sw_down):
        import jax, jax.numpy as jnp
        import numpy as np
        B, S, H = (2, 128, 256)
        E, K, F = (8, 2, 176)
        N_SHARED = 2
        FS = F * N_SHARED
        ROUTED_SCALE = 1.0

        def _swiglu_mlp(x, wg, wu, wd):
            return jax.nn.silu(x @ wg.T) * (x @ wu.T) @ wd.T
        b, s, h = hidden_states.shape
        x = hidden_states.reshape(-1, h)
        T = x.shape[0]
        logits = x.astype(jnp.float32) @ gate_weight.astype(jnp.float32).T
        scores = jax.nn.softmax(logits, axis=-1)
        topk_w, topk_idx = jax.lax.top_k(scores, K)
        topk_w = topk_w / (jnp.sum(topk_w, axis=-1, keepdims=True) + 1e-20)
        topk_w = topk_w * ROUTED_SCALE
        cw = jnp.zeros((T, E), jnp.float32).at[jnp.arange(T)[:, None], topk_idx].add(topk_w)
        g = jax.nn.silu(jnp.einsum('th,efh->tef', x, w_gate)) * jnp.einsum('th,efh->tef', x, w_up)
        expert_out = jnp.einsum('tef,ehf->teh', g, w_down)
        y = jnp.einsum('te,teh->th', cw, expert_out).reshape(b, s, h)
        y = y + _swiglu_mlp(x, sw_gate, sw_up, sw_down).reshape(b, s, h)
        return y
    x = L0_attn_x
    xn = _layernorm(x, axis=-1)
    x = x + _L0_attn_ref(xn, L0_attn_w_qkv, L0_attn_w_proj, L0_attn_b_proj) + _L0_ffn_ref(xn, L0_ffn_gate_w, L0_ffn_w_gate, L0_ffn_w_up, L0_ffn_w_down)
    xn = _layernorm(x, axis=-1)
    x = x + _L1_attn_ref(xn, L1_attn_W_in, L1_attn_b_in, L1_attn_W_out, L1_attn_b_out, L1_attn_gamma, L1_attn_beta) + _L1_ffn_ref(xn, L1_ffn_gate_weight, L1_ffn_w_gate, L1_ffn_w_up, L1_ffn_w_down, L1_ffn_sw_gate, L1_ffn_sw_up, L1_ffn_sw_down)
    return x

_drawn_inputs = setup_inputs


def setup_inputs(seed=0):
    import zlib

    import numpy as np

    out = dict(_drawn_inputs(seed))
    spreads = {'L1_attn_b_in': (0.0, 0.1),
     'L1_attn_b_out': (0.0, 0.1),
     'L1_attn_gamma': (1.0, 0.2),
     'L1_attn_beta': (0.0, 0.1)}
    factors = {'L0_attn_b_proj': 2.816}
    for name, (base, spread) in spreads.items():
        noise = np.random.default_rng([zlib.crc32(name.encode()), seed]).standard_normal(out[name].shape)
        drawn = base * np.exp(spread * noise) if base else spread * noise
        out[name] = jnp.asarray(drawn.astype(out[name].dtype))
    for name, factor in factors.items():
        out[name] = (out[name] * factor).astype(out[name].dtype)
    return out
```

```python
import concourse.bass as bass
from concourse import mybir
from contextlib import ExitStack


P = 128
BATCH, SEQ, DIM = 4, 512, 256
KD = DIM // P
BLOCKS = SEQ // P
TILES = BLOCKS * BATCH
COLS = BATCH * P
HEAD = 32
EPS_ATTN = 1e-15
EPS_NORM = 1e-5
EPS_TOPK = 1e-20
FE = 176
E0, K0 = 16, 6
E1, K1, SHARED = 8, 2, 2
CH0 = E0 * FE // P
CH1 = -(-(E1 + SHARED) * FE // P)
HIDDEN = 512
KH = HIDDEN // P
LANES = KH * BATCH
W_SCALE = 64.0
H_SCALE = 64.0
Y_DESCALE = 1.0 / (W_SCALE * H_SCALE)

PIECE = 768
QKV, MISC, CHUNK0, REC = 0, 2, 3, 3 + CH0
SLOTS = REC + 3
EARLY = 8
STEPS = 10
HALF = STEPS // 2
TICKS = -(-SEQ // STEPS)
SLOTS_T = TICKS * STEPS
SPLIT_AT = (0, 32, 64)


def build(nc, x, weights, consts, vectors, out):
    f32, f16, bf16, i32 = mybir.dt.float32, mybir.dt.float16, mybir.dt.bfloat16, mybir.dt.int32
    ALU, ACT, AX = mybir.AluOpType, mybir.ActivationFunctionType, mybir.AxisListType
    DS = bass.ds

    ctx = ExitStack()
    with ctx:
        def sb(name, shape, dt=f32):
            return ctx.enter_context(nc.sbuf_tensor(name, shape, dt))

        def sem(name):
            return ctx.enter_context(nc.semaphore(name))

        W = sb("W", [P, SLOTS, 2, PIECE], f16)
        stage = sb("stage", [P, 2, PIECE])
        xres = sb("xres", [P, BLOCKS, BATCH, DIM])
        xT = sb("xT", [P, BLOCKS, KD, 2, COLS], f16)
        US = sb("US", [P, LANES, SLOTS_T + 8])
        ring = sb("ring", [P, STEPS, 2 * LANES])
        state_scaled = sb("state_scaled", [P, 2, LANES, HALF])
        h_scale = sb("h_scale", [P, LANES, HALF])
        zbuf = sb("zbuf", [P, 2 * LANES])
        gam = sb("gam", [P, 2 * LANES])
        scr = sb("scr", [P, 8, COLS])
        hh = sb("hh", [P, 2, COLS], f16)
        hl = sb("hl", [P, 2, COLS], f16)
        oT = sb("oT", [P, KD, 2, COLS], f16)
        BD = sb("BD", [P, BATCH, 2, P])
        DN = sb("DN", [P, BATCH, 2, P])
        sel = sb("sel", [P, CH0, P], bf16)
        cwT = sb("cwT", [P, TILES * P], bf16)
        cst = sb("cst", [P, 2 * P])
        identb = sb("identb", [P, P], bf16)
        vec = sb("vec", [P, 3 * KH + 2 * KD])
        ubias = sb("ubias", [P, KH])
        stats = sb("stats", [P, BATCH, 6])
        mv = sb("mv", [P, BATCH, 2])
        rstd = sb("rstd", [P, BATCH])
        var = sb("var", [P, BATCH])
        half_var = sb("half_var", [P, BATCH])
        guess = sb("guess", [P, BATCH], i32)
        lg1 = sb("lg1", [P, TILES, E1])
        ksum = sb("ksum", [P, BATCH, 2])
        gsm = sb("gsm", [P, 3, TILES])
        ident, mask = cst[:, 0:P], cst[:, P:2 * P]

        sg = [scr[:, 0, :], scr[:, 1, :]]
        h32 = [scr[:, 2, :], scr[:, 3, :]]
        xn = [scr[:, 2 * n:2 * n + 2, :].rearrange("p a (b d) -> p (a b) d", d=DIM) for n in range(2)]
        yT = [scr[:, 4, :], scr[:, 5, :]]
        qT = [scr[:, 0, :], scr[:, 1, :]]
        den = [scr[:, 2, :], scr[:, 3, :]]
        rden = [scr[:, 4, :], scr[:, 5, :]]
        o32 = [scr[:, 6, :], scr[:, 7, :]]
        kr = [scr[:, 2, 0:DIM], scr[:, 3, 0:DIM]]
        vflat = scr[:, 4:6, :].rearrange("p a n -> p (a n)")
        vx = [vflat[:, n * 512:n * 512 + 2 * (P + 1)].rearrange("p (h e) -> p h e", h=2) for n in range(2)]
        EW = 24
        gate_a = [scr[:, 6, 0:TILES * E0].rearrange("p (t e) -> p t e", e=E0),
                  scr[:, 6, 0:TILES * E1].rearrange("p (t e) -> p t e", e=E1)]
        gate_p = scr[:, 7, 0:TILES * EW].rearrange("p (t e) -> p t e", e=EW)
        top8 = scr[:, 6, 256:256 + TILES * 8].rearrange("p (t e) -> p t e", e=8)
        gate_m = sb("gate_m", [P, TILES, EW])
        cw3 = sb("cw3", [P, TILES, P], bf16)
        early = US[:, :, :].rearrange("p a b -> p (a b)")
        US16 = US[:, :, :].rearrange("p a b -> p (a b)").bitcast(f16).rearrange(
            "p (a b two) -> p a b two", a=LANES, two=2)

        def bank(name):
            return ctx.enter_context(nc.psum_tensor(name, [P, 512], f32))
        G = [bank("G0"), bank("G1")]
        U = [bank("U0"), bank("U1")]
        C = [bank("C0"), bank("C1")]
        Y = [bank("Y0"), bank("Y1")]
        cw_bank = [C[0][:, :].bitcast(bf16), C[1][:, :].bitcast(bf16)]

        x_loaded = [sem(f"x_loaded{j}") for j in range(BLOCKS)]
        consts_loaded = sem("consts_loaded")
        early_loaded = [sem(f"early_loaded{s}") for s in range(EARLY)]
        stage_loaded = [sem("stage_loaded0"), sem("stage_loaded1")]
        heads_split = sem("heads_split")
        pieces_split = sem("pieces_split")
        sel_made = sem("sel_made")
        dve_order = sem("dve_order")
        pool_order = sem("pool_order")
        consts_made = sem("consts_made")
        xn_done = sem("xn_done")
        xn_turned = sem("xn_turned")
        xhead_done = sem("xhead_done")
        xtail_done = sem("xtail_done")
        logits_done = sem("logits_done")
        logits_kept = sem("logits_kept")
        shifted_done = sem("shifted_done")
        exp_done = sem("exp_done")
        cw_done = sem("cw_done")
        cw_turned = sem("cw_turned")
        cwT_done = sem("cwT_done")
        kv_done = sem("kv_done")
        kv_copied = sem("kv_copied")
        kvsum_done = sem("kvsum_done")
        kvsum_banks_free = sem("kvsum_banks_free")
        ksum_kept = sem("ksum_kept")
        kvsum_masked = sem("kvsum_masked")
        q_done = sem("q_done")
        q_copied = sem("q_copied")
        numden_done = sem("numden_done")
        o_done = sem("o_done")
        ohead_done = sem("ohead_done")
        otail_done = sem("otail_done")
        gate_done = sem("gate_done")
        up_done = sem("up_done")
        silu_done = sem("silu_done")
        gated_done = sem("gated_done")
        h_done = sem("h_done")
        hhead_done = sem("hhead_done")
        htail_done = sem("htail_done")
        down_done = sem("down_done")
        y_copied = sem("y_copied")
        y_turned = sem("y_turned")
        x_added = sem("x_added")
        u_done = sem("u_done")
        u_copied = sem("u_copied")
        u_in_ring = sem("u_in_ring")
        z_done = sem("z_done")
        state_done = sem("state_done")
        state_copied = sem("state_copied")
        state_head = sem("state_head")
        states_out = sem("states_out")
        out_stored = sem("out_stored")

        PHASES = [(0, j) for j in range(BLOCKS)] + [(1, j) for j in range(BLOCKS)]
        CHUNKS = (CH0, CH1)

        def chunks_before(layer, j):
            return j * CH0 if layer == 0 else BLOCKS * CH0 + j * CH1

        def layer_of_piece(layer, j):
            return 0 if (layer, j) == (0, 0) else 1

        def tick0(layer, j):
            if layer == 0:
                return (j - 1) * (CH0 // 2) if j else None
            return (BLOCKS - 1) * (CH0 // 2) + j * (CH1 // 2)

        def loads(layer, j, k):
            if (layer, j) == (0, 0) and k < (SLOTS - EARLY) // 2:
                return EARLY // 2, 0
            if (layer, j) == (0, BLOCKS - 1) and k >= CH0 // 2 - CH1 // 2:
                return SLOTS // 2, CH0 // 2 - CH1 // 2
            return None

        def segments(layer, j):
            pairs = CHUNKS[layer] // 2
            kinds = []
            for k in range(pairs):
                t0 = tick0(layer, j)
                kinds.append((t0 is not None and t0 + k < TICKS, loads(layer, j, k)))
            cuts, out_ = [0, 1], []
            for k in range(2, pairs):
                if kinds[k] != kinds[k - 1]:
                    cuts.append(k)
            cuts.append(pairs)
            for a, b in zip(cuts, cuts[1:]):
                out_.append((a, b) + kinds[a])
            return out_

        def over_pairs(eng, layer, j, body):
            for a, b, steps, load in segments(layer, j):
                def run(k, a=a, steps=steps, load=load):
                    body(k, a == 0, tick0(layer, j) + k if steps else None,
                         load[0] + (k - load[1]) if load else None)
                if b - a == 1:
                    run(a)
                else:
                    with eng.Fori(a, b) as k:
                        run(k)

        def states_ready(t):
            return 2 * (t // STEPS) + (1 if t % STEPS < HALF else 2)

        def turn_banks(i):
            return (G if i % 2 == 0 else U) if i < BLOCKS else U

        block = ctx.enter_context(nc.Block())

        @block.sync
        def _(sp):
            for s in range(EARLY):
                sp.dma_start(early[:, s * PIECE:(s + 1) * PIECE], weights[s, :, :]).then_inc(early_loaded[s], 16)
            for a in range(2):
                sp.dma_start(stage[:, a, :], weights[EARLY + a, :, :]).then_inc(stage_loaded[a], 16)
            with sp.Fori(EARLY // 2 + 1, (SLOTS + CH1) // 2) as r:
                for a in range(2):
                    sp.wait_ge(pieces_split, 2 * r + a - 1)
                    sp.dma_start(stage[:, a, :], weights[DS(2 * r + a, 1), :, :].rearrange("o p n -> (o p) n"))\
                      .then_inc(stage_loaded[a], 16)
            for j in range(BLOCKS):
                for half in range(2):
                    sp.wait_ge(x_added, 2 * (BLOCKS + j) + half + 1)
                    sp.dma_start(out[2 * half:2 * half + 2, P * j:P * j + P, :].rearrange("b t d -> t b d"),
                                 xres[:, j, 2 * half:2 * half + 2, :]).then_inc(out_stored, 16)
            sp.wait_ge(out_stored, 16 * 2 * BLOCKS)

        @block.tensor
        def _(pe):
            def weight(slot, part, off, cols=P):
                return W[:, DS(slot, 1), part, off:off + cols].rearrange("p o n -> p (o n)")

            PRODUCTS = ((0, 0), (0, 1), (1, 0))

            def split_product(bank, terms, start=True, stop=True):
                n, count = 0, len(PRODUCTS) * len(terms)
                for w, act in terms:
                    for wp, ap in PRODUCTS:
                        last = nc.tensor.matmul(bank, w(wp), act(ap), start=start and n == 0,
                                                stop=stop and n == count - 1)
                        n += 1
                return last

            def turn_xn(i):
                banks = turn_banks(i)
                pe.wait_ge(xn_done, BATCH * (i + 1))
                for b in range(BATCH):
                    for kd in range(KD):
                        last = nc.tensor.transpose(banks[kd][:, b * P:(b + 1) * P],
                                                   xn[i % 2][:, b, kd * P:(kd + 1) * P], ident)
                last.then_inc(xn_turned, 1)

            def logits(bank, j, b, gate_off, experts):
                n = 0
                for kd in range(KD):
                    for xp in range(2):
                        for wp in range(2):
                            last = nc.tensor.matmul(
                                bank, xT[:, DS(j, 1), kd, xp, b * P:(b + 1) * P].rearrange("p o n -> p (o n)"),
                                W[:, MISC, wp, gate_off + kd * experts:gate_off + (kd + 1) * experts],
                                start=n == 0, stop=n == 4 * KD - 1)
                            n += 1
                return last

            def turn_cw(layer):
                pe.wait_ge(cw_done, layer + 1)
                for t in range(TILES):
                    last = nc.tensor.transpose(cw_bank[t // 8][:, (t % 8) * P:(t % 8 + 1) * P], cw3[:, t, :], identb[:, :])
                last.then_inc(cw_turned, 1)

            pe.wait_ge(consts_loaded, 32)
            for i in range(BLOCKS):
                if i >= 2:
                    pe.wait_ge(xtail_done, KD * (i - 1))
                turn_xn(i)
            pe.wait_ge(xtail_done, KD * BLOCKS)
            pe.wait_ge(pieces_split, CHUNK0)
            with pe.Fori(0, BLOCKS) as j:
                for b in range(BATCH):
                    lg = C[0][:, DS(j * BATCH * E0 + b * E0, E0)]
                    logits(lg, j, b, 2 * DIM, E0).then_inc(logits_done, 1)

            pe.wait_ge(kvsum_banks_free, 1)
            with pe.Fori(0, BATCH) as b:
                def keys_values(j):
                    if j >= 2:
                        pe.wait_ge(kv_copied, BLOCKS * b + j - 1)
                    split_product(G[j % 2][:, :], [
                        (lambda p_, kd=kd: xT[:, j, kd, p_, DS(b * P, P)],
                         lambda p_, kd=kd: W[:, QKV + kd, p_, DIM:3 * DIM]) for kd in range(KD)])\
                        .then_inc(kv_done, 1)

                def add_keys_values(j):
                    pe.wait_ge(kv_copied, BLOCKS * b + j + 1)
                    for h in range(2):
                        last = nc.tensor.matmul(U[h][:, 0:P + 1], kr[j % 2][:, h * P:(h + 1) * P], vx[j % 2][:, h, :],
                                                start=j == 0, stop=j == BLOCKS - 1)
                    return last

                keys_values(0)
                for j in range(1, BLOCKS):
                    keys_values(j)
                    if j == 1:
                        pe.wait_ge(kvsum_banks_free, 2 * b + 1)
                    add_keys_values(j - 1)
                add_keys_values(BLOCKS - 1).then_inc(kvsum_done, 1)
            turn_cw(0)

            def attention(j):
                if j == 0:
                    pe.wait_ge(kvsum_masked, 2 * BATCH)
                    pe.wait_ge(cwT_done, 2)
                else:
                    pe.wait_ge(u_copied, KH * j)
                    pe.wait_ge(logits_kept, j)
                for h in range(2):
                    split_product(G[h][:, :], [
                        (lambda p_, kd=kd: W[:, QKV + kd, p_, h * P:(h + 1) * P],
                         lambda p_, kd=kd: xT[:, j, kd, p_, :]) for kd in range(KD)]).then_inc(q_done, 1)
                for h in range(2):
                    pe.wait_ge(q_copied, 2 * j + h + 1)
                    for b in range(BATCH):
                        cols = slice(b * P, (b + 1) * P)
                        nc.tensor.matmul(U[h][:, cols], BD[:, b, h, :], qT[h][:, cols], start=True, stop=True)
                    for b in range(BATCH):
                        cols = slice(b * P, (b + 1) * P)
                        last = nc.tensor.matmul(C[h][:, cols], DN[:, b, h, :], qT[h][:, cols], start=True, stop=True)
                    last.then_inc(numden_done, 1)
                pe.wait_ge(otail_done, 2 * (j + 1))
                for dh in range(KD):
                    split_product(Y[dh][:, :], [
                        (lambda p_, h=h: W[:, MISC, p_, h * DIM + dh * P:h * DIM + (dh + 1) * P],
                         lambda p_, h=h: oT[:, h, p_, :]) for h in range(2)], stop=False)

            def state_product(j):
                pe.wait_ge(states_out, states_ready(P * (j + 1)))
                pe.wait_ge(y_copied, KD * (BLOCKS + j))
                for dh in range(KD):
                    def w_out(c, dh=dh):
                        slot, off = (REC + c, HIDDEN) if c < 2 else (REC + 2, (c - 2) * DIM)
                        return lambda p_: W[:, slot, p_, off + dh * P:off + (dh + 1) * P]
                    split_product(Y[dh][:, :], [
                        (w_out(c), lambda p_, c=c: US16[:, BATCH * c:BATCH * (c + 1), P * j + 1:P * j + P + 1, p_])
                        for c in range(KH)], stop=False)

            def gate_up(layer, j, c, a, first, piece_wait):
                n = chunks_before(layer, j) + c
                slot = CHUNK0 + c
                if piece_wait:
                    pe.wait_ge(pieces_split, c + CHUNK0 + 1)
                if not first:
                    pe.wait_ge(silu_done, n - 1)
                for bank, off, done in ((G[a], 0, gate_done), (U[a], KD * P, None)):
                    if done is None and not first:
                        pe.wait_ge(h_done, n - 1)
                    last = split_product(bank[:, :], [
                        (lambda p_, kd=kd: weight(slot, p_, off + kd * P),
                         lambda p_, kd=kd: xT[:, j, kd, p_, :]) for kd in range(KD)])
                    if done is not None:
                        last.then_inc(done, 1)
                nc.tensor.matmul(C[a][:, :], sel[:, DS(c, 1), :].rearrange("p o n -> p (o n)"),
                                 cwT[:, j * COLS:(j + 1) * COLS], start=True, stop=True).then_inc(up_done, 1)

            def down(layer, j, c, a, stop=False):
                n = chunks_before(layer, j) + c
                pe.wait_ge(htail_done, n + 1)
                act = (hh, hl)
                for dh in range(KD):
                    last = split_product(Y[dh][:, :], [
                        (lambda p_: weight(CHUNK0 + c, p_, 2 * KD * P + dh * P), lambda p_: act[p_][:, a, :])],
                        start=False, stop=stop)
                last.then_inc(down_done, 1)

            for phase, (layer, j) in enumerate(PHASES):
                if layer == 0:
                    attention(j)
                    if j == 0:
                        pe.wait_ge(sel_made, 6)
                else:
                    if j == 0:
                        pe.wait_ge(u_copied, KH * BLOCKS)
                        turn_cw(1)
                        pe.wait_ge(cwT_done, 4)
                        pe.wait_ge(logits_kept, BLOCKS)
                        pe.wait_ge(pieces_split, SLOTS + CH1)
                    else:
                        pe.wait_ge(x_added, 2 * phase)
                    state_product(j)

                def pair(k, first, tick, piece):
                    for a in range(2):
                        gate_up(layer, j, 2 * k + a, a, first, (layer, j) == (0, 0))
                        if not first:
                            down(layer, j, 2 * k + a - 2, a)
                over_pairs(pe, layer, j, pair)
                for a in range(2):
                    down(layer, j, CHUNKS[layer] - 2 + a, a, stop=a == 1)

                for half in range(2):
                    if half == 0:
                        pe.wait_ge(y_copied, KD * (phase + 1))
                    for b in range(2):
                        for dh in range(KD):
                            last = nc.tensor.transpose(G[half][:, b * DIM + dh * P:b * DIM + (dh + 1) * P],
                                                       yT[dh][:, (2 * half + b) * P:(2 * half + b + 1) * P], ident)
                    last.then_inc(y_turned, 1)
                if layer == 0:
                    turn_xn(BLOCKS + j)
                    pe.wait_ge(xtail_done, KD * (BLOCKS + j + 1))
                    if j == 0:
                        pe.wait_ge(pieces_split, SLOTS)
                    for c in range(KH):
                        split_product((G + C)[c][:, :], [
                            (lambda p_, kd=kd: W[:, REC + kd, p_, c * P:(c + 1) * P],
                             lambda p_, kd=kd: xT[:, j, kd, p_, :]) for kd in range(KD)]).then_inc(u_done, 1)
                    for b in range(BATCH):
                        last = logits(U[0][:, b * E1:(b + 1) * E1], j, b, 2 * DIM + KD * E0, E1)
                    last.then_inc(logits_done, 1)

        @block.scalar
        def _(act):
            for j in range(BLOCKS):
                act.dma_start(xres[:, j, :, :], x[:, P * j:P * j + P, :].rearrange("b t d -> t b d"))\
                   .then_inc(x_loaded[j], 16)
                if j == 0:
                    act.dma_start(cst[:, :], consts).then_inc(consts_loaded, 16)
                    act.dma_start(vec[:, :], vectors).then_inc(consts_loaded, 16)

            def split_head(s, src):
                nc.scalar.activation(W[:, DS(s, 1), 0, :].rearrange("p o n -> p (o n)"), src, ACT.Copy,
                                     scale=W_SCALE).then_inc(heads_split, 1)

            def split_early(s):
                act.wait_ge(early_loaded[s], 16)
                split_head(s, early[:, s * PIECE:(s + 1) * PIECE])

            def split_staged(layer, r, a):
                act.wait_ge(stage_loaded[a], 16 * (r - EARLY // 2 + 1))
                if layer == 0:
                    split_head(2 * r + a, stage[:, a, :])
                else:
                    act.wait_ge(down_done, (BLOCKS - 1) * CH0 + 2 * r + a - SLOTS + 1)
                    split_head(2 * r + a - SLOTS + CHUNK0, stage[:, a, :])

            def x_heads(i):
                act.wait_ge(xn_turned, i + 1)
                for kd in range(KD):
                    nc.scalar.activation(xT[:, i % BLOCKS, kd, 0, :], turn_banks(i)[kd][:, :], ACT.Copy)\
                      .then_inc(xhead_done, 1)

            def gate_exp(layer):
                act.wait_ge(shifted_done, layer + 1)
                nc.scalar.activation(gate_a[layer], gate_a[layer], ACT.Exp, scale=1.0 / W_SCALE).then_inc(exp_done, 1)

            def copy_cwT(layer):
                act.wait_ge(cw_turned, layer + 1)
                for half in range(2):
                    nc.scalar.activation(cwT[:, half * 8 * P:(half + 1) * 8 * P], cw_bank[half], ACT.Copy)\
                      .then_inc(cwT_done, 1)

            x_heads(0)
            for s in range(CHUNK0):
                split_early(s)
            for i in range(1, BLOCKS):
                x_heads(i)
            gate_exp(0)
            act.wait_ge(consts_made, 1)
            with act.Fori(0, BATCH) as b:
                for j in range(BLOCKS):
                    act.wait_ge(kv_done, BLOCKS * b + j + 1)
                    nc.scalar.activation(kr[j % 2], G[j % 2][:, 0:DIM], ACT.Relu, scale=1.0 / W_SCALE)
                    nc.scalar.activation(vx[j % 2][:, :, 0:P], G[j % 2][:, DIM:2 * DIM].rearrange("p (h e) -> p h e", h=2),
                                         ACT.Copy, scale=1.0 / W_SCALE).then_inc(kv_copied, 1)
            for s in range(CHUNK0, EARLY):
                split_early(s)
            copy_cwT(0)

            def attention(j):
                for h in range(2):
                    act.wait_ge(q_done, 2 * j + h + 1)
                    nc.scalar.activation(qT[h], G[h][:, :], ACT.Relu, scale=1.0 / W_SCALE).then_inc(q_copied, 1)
                for h in range(2):
                    act.wait_ge(o_done, 2 * j + h + 1)
                    nc.scalar.activation(oT[:, h, 0, :], o32[h], ACT.Copy).then_inc(ohead_done, 1)

            def silu(n, a, first):
                act.wait_ge(gate_done, n + 1)
                if not first:
                    act.wait_ge(gated_done, n - 1)
                nc.scalar.activation(sg[a], G[a][:, :], ACT.Silu, scale=1.0 / W_SCALE).then_inc(silu_done, 1)

            def h_head(n, a):
                act.wait_ge(h_done, n + 1)
                nc.scalar.activation(hh[:, a, :], h32[a], ACT.Copy).then_inc(hhead_done, 1)

            def step(tick, i):
                if tick is None:
                    return
                if i == HALF - 1 and not (isinstance(tick, int) and tick == 0):
                    act.wait_ge(states_out, 2 * tick)
                if i == STEPS - 1:
                    act.wait_ge(states_out, 2 * tick + 1)
                act.wait_ge(z_done, STEPS * tick + i + 1)
                nc.scalar.activation(ring[:, (i + 1) % STEPS, 0::2], zbuf[:, 1::2], ACT.Tanh).then_inc(state_done, 1)

            for phase, (layer, j) in enumerate(PHASES):
                n0 = chunks_before(layer, j)
                if layer == 0:
                    attention(j)
                elif j == 0:
                    gate_exp(1)
                    copy_cwT(1)
                if (layer, j) == (0, 1):
                    act.wait_ge(consts_made, 1)
                    nc.scalar.activation(ring[:, 0, 0::2], gam[:, 0::2], ACT.Copy).then_inc(state_done, 1)

                def pair(k, first, tick, piece):
                    n = n0 + 2 * k
                    step(tick, 0)
                    silu(n, 0, first)
                    step(tick, 1)
                    step(tick, 2)
                    if not first:
                        h_head(n - 1, 1)
                    step(tick, 3)
                    step(tick, 4)
                    step(tick, 5)
                    silu(n + 1, 1, first)
                    step(tick, 6)
                    step(tick, 7)
                    h_head(n, 0)
                    step(tick, 8)
                    step(tick, 9)
                    if piece is not None:
                        for a in range(2):
                            split_staged(layer_of_piece(layer, j), piece, a)
                over_pairs(act, layer, j, pair)
                act.wait_ge(down_done, n0 + CHUNKS[layer] - 2)
                h_head(n0 + CHUNKS[layer] - 1, 1)

                act.wait_ge(down_done, chunks_before(layer, j) + CHUNKS[layer])
                for dh in range(KD):
                    bias = vec[:, 3 * KH + layer * KD + dh:3 * KH + layer * KD + dh + 1]
                    nc.scalar.activation(yT[dh], Y[dh][:, :], ACT.Identity, bias=bias, scale=Y_DESCALE).then_inc(y_copied, 1)
                if layer == 0:
                    x_heads(BLOCKS + j)
                    for c in range(KH):
                        act.wait_ge(u_done, KH * j + c + 1)
                        nc.scalar.activation(US[:, BATCH * c:BATCH * (c + 1), P * j:P * (j + 1)],
                                             (G + C)[c][:, :].rearrange("p (b t) -> p b t", b=BATCH), ACT.Identity,
                                             bias=ubias[:, c:c + 1], scale=1.0 / W_SCALE).then_inc(u_copied, 1)
                    act.wait_ge(logits_done, TILES + j + 1)
                    nc.scalar.activation(lg1[:, BATCH * j:BATCH * (j + 1), :],
                                         U[0][:, 0:BATCH * E1].rearrange("p (b e) -> p b e", b=BATCH), ACT.Copy)\
                      .then_inc(logits_kept, 1)

        @block.vector
        def _(dve):
            ordered = [0]

            def mark(ins):
                ordered[0] += 1
                return ins.then_inc(dve_order, 1)

            def settle():
                dve.wait_ge(dve_order, ordered[0])

            def layer_norm(i):
                j, buf = i % BLOCKS, xn[i % 2]
                if i < BLOCKS:
                    dve.wait_ge(x_loaded[j], 16)
                settle()
                for b in range(BATCH):
                    mark(nc.vector.bn_stats(stats[:, b, :], xres[:, j, b, :]))
                settle()
                for b in range(BATCH):
                    mark(nc.vector.bn_aggr(mv[:, b, :], stats[:, b, :]))
                settle()
                mark(nc.vector.tensor_scalar(var[:, :], mv[:, :, 1], EPS_NORM, None, ALU.add))
                settle()
                mark(nc.vector.tensor_scalar(guess[:, :], var[:, :].bitcast(i32), 1, None, ALU.logical_shift_right))
                mark(nc.vector.tensor_scalar(half_var[:, :], var[:, :], -0.5, None, ALU.mult))
                settle()
                mark(nc.vector.tensor_scalar(rstd[:, :].bitcast(i32), guess[:, :], -1.0, float(0x5F3759DF), ALU.mult, ALU.add))
                settle()
                for _ in range(3):
                    mark(nc.vector.tensor_tensor(var[:, :], rstd[:, :], rstd[:, :], ALU.mult))
                    settle()
                    mark(nc.vector.tensor_tensor(var[:, :], var[:, :], half_var[:, :], ALU.mult))
                    settle()
                    mark(nc.vector.scalar_tensor_tensor(out=rstd[:, :], in0=var[:, :], scalar=1.5, in1=rstd[:, :],
                                                        op0=ALU.add, op1=ALU.mult))
                    settle()
                if i >= 2:
                    dve.wait_ge(xn_turned, i - 1)
                for b in range(BATCH):
                    nc.vector.tensor_scalar(buf[:, b, :], xres[:, j, b, :], mv[:, b, 0:1], rstd[:, b:b + 1],
                                            ALU.subtract, ALU.mult).then_inc(xn_done, 1)

            def x_tails(i):
                for kd in range(KD):
                    dve.wait_ge(xhead_done, KD * i + kd + 1)
                    nc.vector.tensor_tensor(xT[:, i % BLOCKS, kd, 1, :], turn_banks(i)[kd][:, :],
                                            xT[:, i % BLOCKS, kd, 0, :], ALU.subtract).then_inc(xtail_done, 1)

            def split_tail(s, count, src):
                dve.wait_ge(heads_split, count + 1)
                dst = W[:, DS(s, 1), :, :].rearrange("p o h n -> p (o h) n")
                nc.vector.scalar_tensor_tensor(out=dst[:, 1, :], in0=src, scalar=W_SCALE, in1=dst[:, 0, :],
                                               op0=ALU.mult, op1=ALU.subtract).then_inc(pieces_split, 1)

            def routing(layer):
                E, K = ((E0, K0), (E1, K1))[layer]
                g = gate_a[layer]
                rest = 8 - K
                if layer == 0:
                    dve.wait_ge(logits_done, TILES)
                    lg = C[0][:, 0:TILES * E0].rearrange("p (t e) -> p t e", e=E0)
                else:
                    dve.wait_ge(logits_kept, BLOCKS)
                    lg = lg1[:, :, :]
                settle()
                mark(nc.vector.memset(cw3[:, :, :], 0.0))
                mark(nc.vector.memset(gate_p[:, :, E:E + rest], -1.0))
                mark(nc.vector.tensor_reduce(gsm[:, 0, :], lg, AX.X, ALU.max))
                settle()
                spread = [P, TILES, E]
                nc.vector.tensor_tensor(g, lg, gsm[:, 0, :].unsqueeze(2).broadcast_to(spread), ALU.subtract)\
                  .then_inc(shifted_done, 1)
                dve.wait_ge(exp_done, layer + 1)
                mark(nc.vector.tensor_reduce(gsm[:, 1, :], g, AX.X, ALU.add))
                settle()
                mark(nc.vector.reciprocal(gsm[:, 2, :], gsm[:, 1, :]))
                settle()
                p = gate_p[:, :, 0:E]
                mark(nc.vector.tensor_tensor(p, g, gsm[:, 2, :].unsqueeze(2).broadcast_to(spread), ALU.mult))
                settle()
                for t in range(TILES):
                    mark(nc.vector.max(top8[:, t, :], gate_p[:, t, 0:E]))
                settle()
                mark(nc.vector.memset(top8[:, :, K:8], -1.0))
                settle()
                for t in range(TILES):
                    mark(nc.vector.match_replace(out=gate_m[:, t, 0:E + rest], in_to_replace=top8[:, t, :],
                                                 in_values=gate_p[:, t, 0:E + rest], imm_value=0.0))
                settle()
                cw = gate_m[:, :, 0:E]
                mark(nc.vector.tensor_tensor(cw, p, cw, ALU.subtract))
                settle()
                if layer == 1:
                    mark(nc.vector.tensor_reduce(gsm[:, 0, :], cw, AX.X, ALU.add))
                    settle()
                    mark(nc.vector.tensor_scalar(gsm[:, 0, :], gsm[:, 0, :], EPS_TOPK, None, ALU.add))
                    settle()
                    mark(nc.vector.reciprocal(gsm[:, 1, :], gsm[:, 0, :]))
                    settle()
                    mark(nc.vector.tensor_tensor(cw, cw, gsm[:, 1, :].unsqueeze(2).broadcast_to(spread), ALU.mult))
                    mark(nc.vector.memset(cw3[:, :, E:E + SHARED], 1.0))
                    settle()
                for part, at in enumerate(SPLIT_AT):
                    piece = cw3[:, :, at:at + E]
                    if part == 2:
                        nc.vector.tensor_copy(piece, cw).then_inc(cw_done, 1)
                        break
                    mark(nc.vector.tensor_copy(piece, cw))
                    settle()
                    mark(nc.vector.tensor_tensor(cw, cw, piece, ALU.subtract))
                    settle()

            mark(nc.vector.memset(gam[:, :], 0.0))
            dve.wait_ge(consts_loaded, 32)
            settle()
            for b in range(BATCH):
                mark(nc.vector.tensor_copy(gam[:, :].rearrange("p (c b two) -> p c b two", b=BATCH, two=2)[:, :, b, 1],
                                           vec[:, 0:KH]))
            mark(nc.vector.tensor_tensor(ubias[:, :], vec[:, KH:2 * KH], vec[:, 2 * KH:3 * KH], ALU.add))
            mark(nc.vector.tensor_copy(identb[:, :], ident))
            layer_norm(0)
            layer_norm(1)
            x_tails(0)
            layer_norm(2)
            for s in range(CHUNK0):
                split_tail(s, s, early[:, s * PIECE:(s + 1) * PIECE])
            x_tails(1)
            layer_norm(3)
            x_tails(2)
            x_tails(3)
            dve.wait_ge(xtail_done, KD * BLOCKS)
            for n in range(2):
                mark(nc.vector.memset(vx[n][:, :, P:P + 1], 1.0))
            settle()
            nc.vector.memset(ksum[:, :, :], 0.0).then_inc(kvsum_banks_free, 1)
            dve.wait_ge(kvsum_banks_free, 1)
            mark(nc.vector.tensor_copy(rstd[:, 0:1], gam[:, 0:1]))
            settle()
            nc.vector.tensor_copy(rstd[:, 1:2], gam[:, 0:1]).then_inc(consts_made, 1)
            routing(0)
            with dve.Fori(0, BATCH) as b:
                dve.wait_ge(kvsum_done, b + 1)
                for h in range(2):
                    nc.vector.tensor_copy(ksum[:, DS(b, 1), h], U[h][:, P:P + 1]).then_inc(ksum_kept, 1)
                dve.wait_ge(ksum_kept, 2 * b + 2)
                for h in range(2):
                    nc.vector.tensor_tensor(BD[:, DS(b, 1), h, :].rearrange("p o n -> p (o n)"), U[h][:, 0:P],
                                            mask, ALU.mult).then_inc(kvsum_banks_free, 1)
                for h in range(2):
                    nc.vector.tensor_scalar(DN[:, DS(b, 1), h, :].rearrange("p o n -> p (o n)"), mask,
                                            ksum[:, DS(b, 1), h], None, ALU.mult).then_inc(kvsum_masked, 1)
            for s in range(CHUNK0, EARLY):
                split_tail(s, s, early[:, s * PIECE:(s + 1) * PIECE])

            dve.wait_ge(pieces_split, EARLY)
            mark(nc.vector.memset(US[:, :, SEQ:SLOTS_T + 8], 0.0))

            def attention(j):
                settle()
                for h in range(2):
                    dve.wait_ge(numden_done, 2 * j + h + 1)
                    mark(nc.vector.tensor_scalar(den[h], C[h][:, :], EPS_ATTN, None, ALU.add))
                    settle()
                    mark(nc.vector.reciprocal(rden[h], den[h]))
                    settle()
                    nc.vector.scalar_tensor_tensor(out=o32[h], in0=U[h][:, :], scalar=H_SCALE, in1=rden[h],
                                                   op0=ALU.mult, op1=ALU.mult).then_inc(o_done, 1)
                for h in range(2):
                    dve.wait_ge(ohead_done, 2 * j + h + 1)
                    nc.vector.tensor_tensor(oT[:, h, 1, :], o32[h], oT[:, h, 0, :], ALU.subtract).then_inc(otail_done, 1)

            def step(tick, i):
                if tick is None:
                    return
                if i % HALF == 0:
                    dve.wait_ge(u_in_ring, 2 * tick + i // HALF + 1)
                dve.wait_ge(state_done, STEPS * tick + i + 1)
                nc.vector.tensor_tensor_scan(zbuf[:, :], gam[:, :], ring[:, i, :], 0.0, ALU.mult, ALU.add)\
                  .then_inc(z_done, 1)

            def gated(n, a, first):
                dve.wait_ge(silu_done, n + 1)
                dve.wait_ge(up_done, n + 1)
                if not first:
                    dve.wait_ge(htail_done, n - 1)
                nc.vector.tensor_tensor(h32[a], sg[a], U[a][:, :], ALU.mult).then_inc(gated_done, 1)

            def routed(n, a):
                dve.wait_ge(gated_done, n + 1)
                nc.vector.tensor_tensor(h32[a], h32[a], C[a][:, :], ALU.mult).then_inc(h_done, 1)

            for phase, (layer, j) in enumerate(PHASES):
                n0 = chunks_before(layer, j)
                if layer == 0:
                    attention(j)
                elif j == 0:
                    routing(1)
                    settle()

                def pair(k, first, tick, piece):
                    n = n0 + 2 * k
                    step(tick, 0)
                    gated(n, 0, first)
                    step(tick, 1)
                    step(tick, 2)
                    routed(n, 0)
                    step(tick, 3)
                    step(tick, 4)
                    step(tick, 5)
                    gated(n + 1, 1, first)
                    step(tick, 6)
                    step(tick, 7)
                    routed(n + 1, 1)
                    step(tick, 8)
                    step(tick, 9)
                    if piece is not None:
                        for a in range(2):
                            into = piece * 2 + a - (SLOTS - CHUNK0 if layer_of_piece(layer, j) else 0)
                            split_tail(into, 2 * piece + a, stage[:, a, :])
                over_pairs(dve, layer, j, pair)

                for half in range(2):
                    dve.wait_ge(y_turned, 2 * phase + half + 1)
                    nc.vector.tensor_tensor(xres[:, j, 2 * half:2 * half + 2, :], xres[:, j, 2 * half:2 * half + 2, :],
                                            G[half][:, :].rearrange("p (b d) -> p b d", b=2), ALU.add)\
                      .then_inc(x_added, 1)
                if layer == 0:
                    dve.wait_ge(x_added, 2 * (phase + 1))
                    layer_norm(BLOCKS + j)
                    x_tails(BLOCKS + j)

        @block.gpsimd
        def _(pool):
            nc.gpsimd.memset(h_scale[:, :, :], H_SCALE).then_inc(pool_order, 1)
            nc.gpsimd.memset(sel[:, :, :], 0.0).then_inc(pool_order, 1)
            pool.wait_ge(pool_order, 2)
            for r, at in enumerate(SPLIT_AT):
                rows = sel[at:at + E0, :, :]
                nc.gpsimd.memset(rows, 1.0).then_inc(pool_order, 1)
                pool.wait_ge(pool_order, 3 + r)
                nc.gpsimd.affine_select(out=rows, in_=rows, compare_op=ALU.is_ge, fill=0.0, base=0,
                                        pattern=[[P, CH0], [1, P]], channel_multiplier=-FE).then_inc(sel_made, 1)
                pool.wait_ge(sel_made, 2 * r + 1)
                nc.gpsimd.affine_select(out=rows, in_=rows, compare_op=ALU.is_ge, fill=0.0, base=FE - 1,
                                        pattern=[[-P, CH0], [-1, P]], channel_multiplier=FE).then_inc(sel_made, 1)

            def h_tail(n, a):
                pool.wait_ge(hhead_done, n + 1)
                nc.gpsimd.tensor_tensor(hl[:, a, :], h32[a], hh[:, a, :], ALU.subtract).then_inc(htail_done, 1)

            def ring_u(half):
                return ring[:, half * HALF:(half + 1) * HALF, 1::2].rearrange("p r l -> p l r")

            def ring_states(half):
                return ring[:, half * HALF:(half + 1) * HALF, 0::2].rearrange("p r l -> p l r")

            def take_u(tick, half):
                nc.gpsimd.tensor_copy(ring_u(half), US[:, :, DS(STEPS * tick + half * HALF, HALF)]).then_inc(u_in_ring, 1)

            def keep_states(tick, half):
                span = US16[:, :, DS(STEPS * tick + half * HALF, HALF), :]
                kept = state_scaled[:, half, :, :]
                nc.gpsimd.tensor_tensor(kept, ring_states(half), h_scale[:, :, :], ALU.mult).then_inc(state_copied, 1)
                pool.wait_ge(state_copied, 2 * tick + half + 1)
                nc.gpsimd.tensor_copy(span[:, :, :, 0], kept).then_inc(state_head, 1)
                pool.wait_ge(state_head, 2 * tick + half + 1)
                nc.gpsimd.tensor_tensor(span[:, :, :, 1], kept, span[:, :, :, 0], ALU.subtract)\
                  .then_inc(states_out, 1)

            for phase, (layer, j) in enumerate(PHASES):
                n0 = chunks_before(layer, j)
                if layer == 0 and j:
                    pool.wait_ge(u_copied, KH * j)

                if (layer, j) == (1, 0):
                    pool.wait_ge(u_copied, KH * BLOCKS)

                def pair(k, first, tick, piece):
                    n = n0 + 2 * k
                    if tick is not None:
                        begun = not (isinstance(tick, int) and tick == 0)
                        if begun:
                            pool.wait_ge(state_done, STEPS * (tick - 1) + HALF + 1)
                        take_u(tick, 0)
                        if begun:
                            pool.wait_ge(state_done, STEPS * tick + 1)
                            keep_states(tick - 1, 1)
                        take_u(tick, 1)
                    if not first:
                        h_tail(n - 1, 1)
                    if tick is not None:
                        pool.wait_ge(state_done, STEPS * tick + HALF)
                        keep_states(tick, 0)
                    h_tail(n, 0)
                over_pairs(pool, layer, j, pair)
                h_tail(n0 + CHUNKS[layer] - 1, 1)


def kernel(**inputs):
    import numpy as np
    import concourse.bacc as bacc
    from concourse.bass_utils import run_bass_kernel_spmd

    a = {n: np.asarray(v) for n, v in inputs.items()}

    def over_rows(m):
        t = np.ascontiguousarray(m.T)
        return t.reshape(t.shape[0] // P, P, t.shape[1])

    def chunk_pieces(gates, ups, downs, chunks):
        units = chunks * P
        padded = []
        for m in (gates, ups, downs):
            q = np.zeros((units, DIM), m.dtype)
            q[:m.shape[0]] = m
            padded.append(q)
        res = np.zeros((chunks, P, PIECE), gates.dtype)
        for c in range(chunks):
            rows = slice(c * P, (c + 1) * P)
            for i, m in enumerate(padded[:2]):
                t = over_rows(m[rows])
                for kd in range(KD):
                    res[c, :, (i * KD + kd) * P:(i * KD + kd + 1) * P] = t[kd]
            res[c, :, 2 * KD * P:] = padded[2][rows]
        return res

    def rows_of_down(w):
        return np.swapaxes(w, 1, 2).reshape(-1, DIM)

    qkv = over_rows(a["L0_attn_w_qkv"])
    proj = over_rows(a["L0_attn_w_proj"])
    gate0, gate1 = over_rows(a["L0_ffn_gate_w"]), over_rows(a["L1_ffn_gate_weight"])
    w_in, w_out = over_rows(a["L1_attn_W_in"]), over_rows(a["L1_attn_W_out"])
    misc = np.zeros((P, PIECE), qkv.dtype)
    body = np.concatenate([proj[0], proj[1], gate0[0], gate0[1], gate1[0], gate1[1]], axis=1)
    misc[:, :body.shape[1]] = body
    last = np.zeros((P, PIECE), qkv.dtype)
    last[:, :2 * DIM] = np.concatenate([w_out[2], w_out[3]], axis=1)
    moe0 = chunk_pieces(a["L0_ffn_w_gate"].reshape(-1, DIM), a["L0_ffn_w_up"].reshape(-1, DIM),
                        rows_of_down(a["L0_ffn_w_down"]), CH0)
    moe1 = chunk_pieces(np.concatenate([a["L1_ffn_w_gate"].reshape(-1, DIM), a["L1_ffn_sw_gate"]]),
                        np.concatenate([a["L1_ffn_w_up"].reshape(-1, DIM), a["L1_ffn_sw_up"]]),
                        np.concatenate([rows_of_down(a["L1_ffn_w_down"]), a["L1_ffn_sw_down"].T]), CH1)
    rec = [np.concatenate([w_in[0], w_out[0]], axis=1), np.concatenate([w_in[1], w_out[1]], axis=1), last]
    weights = np.ascontiguousarray(np.concatenate([np.stack([qkv[0], qkv[1], misc]), moe0, np.stack(rec), moe1]))

    def column(v):
        return v.reshape(-1, P).T

    vectors = np.ascontiguousarray(np.concatenate([column(a[n]) for n in (
        "L1_attn_gamma", "L1_attn_beta", "L1_attn_b_in", "L0_attn_b_proj", "L1_attn_b_out")], axis=1))
    consts = np.concatenate([np.eye(P), np.kron(np.eye(P // HEAD), np.ones((HEAD, HEAD)))], axis=1).astype(np.float32)
    x = np.ascontiguousarray(a["L0_attn_x"])

    nc = bacc.Bacc("TRN2", target_bir_lowering=False, num_devices=1)
    f32 = mybir.dt.float32
    arrays = {"x": x, "weights": weights, "consts": consts, "vectors": vectors}
    aps = [nc.dram_tensor(n, v.shape, f32, kind="ExternalInput").ap() for n, v in arrays.items()]
    out = nc.dram_tensor("out", x.shape, f32, kind="ExternalOutput").ap()
    build(nc, *aps, out)
    r = run_bass_kernel_spmd(nc, [arrays], core_ids=[0])
    return r.results[0]["out"]
```

```python
import concourse.bass as bass
from concourse import mybir
from contextlib import ExitStack


P = 128
BATCH, SEQ, DIM = 4, 512, 256
KD = DIM // P
BLOCKS = SEQ // P
TILES = BLOCKS * BATCH
COLS = BATCH * P
HEAD = 32
EPS_ATTN = 1e-15
EPS_NORM = 1e-5
EPS_TOPK = 1e-20
FE = 176
E0, K0 = 16, 6
E1, K1, SHARED = 8, 2, 2
CH0 = E0 * FE // P
CH1 = -(-(E1 + SHARED) * FE // P)
CHUNKS = (CH0, CH1)
HIDDEN = 512
KH = HIDDEN // P
LANES = KH * BATCH
W_SCALE = 64.0
H_SCALE = 64.0
Y_DESCALE = 1.0 / (W_SCALE * H_SCALE)

PIECE = 768
QKV, MISC, CHUNK0, REC = 0, 2, 3, 3 + CH0
SLOTS = REC + 3
EARLY = 8
STEPS = 10
HALF = STEPS // 2
TICKS = -(-SEQ // STEPS)
SLOTS_T = TICKS * STEPS
SPLIT_AT = (0, 32, 64)


def build(nc, x, weights, consts, vectors, out):
    f32, f16, bf16, i32 = mybir.dt.float32, mybir.dt.float16, mybir.dt.bfloat16, mybir.dt.int32
    ALU, ACT, AX = mybir.AluOpType, mybir.ActivationFunctionType, mybir.AxisListType
    DS = bass.ds

    ctx = ExitStack()
    with ctx:
        def sb(name, shape, dt=f32):
            return ctx.enter_context(nc.sbuf_tensor(name, shape, dt))

        def sem(name):
            return ctx.enter_context(nc.semaphore(name))

        W = sb("W", [P, SLOTS, 2, PIECE], f16)
        stage = sb("stage", [P, 2, PIECE])
        xres = sb("xres", [P, BLOCKS, BATCH, DIM])
        xT = sb("xT", [P, BLOCKS, KD, 2, COLS], f16)
        US = sb("US", [P, LANES, SLOTS_T + 8])
        ring = sb("ring", [P, STEPS, 2 * LANES])
        state_scaled = sb("state_scaled", [P, 2, LANES, HALF])
        h_scale = sb("h_scale", [P, LANES, HALF])
        zbuf = sb("zbuf", [P, 2 * LANES])
        gam = sb("gam", [P, 2 * LANES])
        scr = sb("scr", [P, 8, COLS])
        hh = sb("hh", [P, 2, COLS], f16)
        hl = sb("hl", [P, 2, COLS], f16)
        BD = sb("BD", [P, BATCH, 2, P])
        KS = sb("KS", [P, BATCH, 2, P // HEAD])
        rden = sb("rden", [P, BATCH * DIM // HEAD])
        zeros = sb("zeros", [P, COLS], bf16)
        sel = sb("sel", [P, CH0, P], bf16)
        cwT = sb("cwT", [P, 2, BLOCKS, COLS], bf16)
        cst = sb("cst", [P, 2 * P])
        identb = sb("identb", [P, P], bf16)
        vec = sb("vec", [P, 3 * KH + 2 * KD])
        ubias = sb("ubias", [P, KH])
        stats = sb("stats", [P, BATCH, 6])
        mv = sb("mv", [P, BATCH, 2])
        rstd = sb("rstd", [P, BATCH])
        var = sb("var", [P, BATCH])
        half_var = sb("half_var", [P, BATCH])
        guess = sb("guess", [P, BATCH], i32)
        gmax = sb("gmax", [P, BATCH])
        gsum = sb("gsum", [P, 2, BATCH])
        gexp = sb("gexp", [P, BLOCKS, BATCH, E0])
        gprob = sb("gprob", [P, BATCH, E0 + 8])
        grest = sb("grest", [P, BATCH, E0 + 8])
        gtop = sb("gtop", [P, BATCH, 8])
        cw3 = sb("cw3", [P, BATCH, P], bf16)
        ident, mask = cst[:, 0:P], cst[:, P:2 * P]


        def scratch(n, dt=f32):
            return scr[:, n:n + 2, :].rearrange("p a n -> p (a n)").bitcast(dt)
        sg = [scr[:, 0, :], scr[:, 1, :]]
        h32 = [scr[:, 2, :], scr[:, 3, :]]
        kr = [scr[:, 0, 0:DIM], scr[:, 1, 0:DIM]]
        vx = [scr[:, 2 + n, 0:2 * (P + 1)].rearrange("p (h e) -> p h e", h=2) 
              for n in range(2)]
        xn = scratch(4).rearrange("p (b d) -> p b d", b=BATCH)
        qT = [scr[:, 4, :], scr[:, 5, :]]
        oT = scratch(4, f16).rearrange("p (h two n) -> p h two n", h=2, two=2)
        yT = [scr[:, 6, :], scr[:, 7, :]]
        otok = scratch(6).rearrange("p (b d) -> p b d", b=BATCH)
        early = US[:, :, :].rearrange("p a b -> p (a b)")
        US16 = US[:, :, :].rearrange("p a b -> p (a b)").bitcast(f16).rearrange(
            "p (a b two) -> p a b two", a=LANES, two=2)

        def bank(name):
            return ctx.enter_context(nc.psum_tensor(name, [P, 512], f32))
        G = bank("G")
        U = [bank("U0"), bank("U1")]
        C = bank("C")
        Y = [[bank("Y00"), bank("Y01")], [bank("Y10"), bank("Y11")]]
        SUM = P + 1
        kvsum = [(Y[0] + [G])[g // 3][:, (g % 3) * SUM:(g % 3 + 1) * SUM] for g in range(2 * BATCH)]

        x_loaded = [sem(f"x_loaded{j}") for j in range(BLOCKS)]
        consts_loaded = sem("consts_loaded")
        early_loaded = [sem(f"early_loaded{s}") for s in range(EARLY)]
        stage_loaded = [sem("stage_loaded0"), sem("stage_loaded1")]
        heads_split = sem("heads_split")
        pieces_split = sem("pieces_split")
        sel_made = sem("sel_made")
        zeros_made = sem("zeros_made")
        ones_made = sem("ones_made")
        dve_order = sem("dve_order")
        pool_order = sem("pool_order")
        xn_done = sem("xn_done")
        xn_turned = sem("xn_turned")
        xhead_done = sem("xhead_done")
        xtail_done = sem("xtail_done")
        logits_done = sem("logits_done")
        shifted_done = sem("shifted_done")
        exp_done = sem("exp_done")
        cw_done = sem("cw_done")
        cw_turned = sem("cw_turned")
        cwT_done = sem("cwT_done")
        kv_done = sem("kv_done")
        kv_copied = sem("kv_copied")
        kvsum_done = sem("kvsum_done")
        kvsum_masked = sem("kvsum_masked")
        q_done = sem("q_done")
        q_copied = sem("q_copied")
        den_done = sem("den_done")
        rden_done = sem("rden_done")
        num_done = sem("num_done")
        o_done = sem("o_done")
        o_turned = sem("o_turned")
        ohead_done = sem("ohead_done")
        otail_done = sem("otail_done")
        gate_done = sem("gate_done")
        up_done = sem("up_done")
        spread_done = sem("spread_done")
        silu_done = sem("silu_done")
        gated_done = sem("gated_done")
        h_done = sem("h_done")
        hhead_done = sem("hhead_done")
        htail_done = sem("htail_done")
        down_done = sem("down_done")
        y_copied = sem("y_copied")
        y_turned = sem("y_turned")
        x_added = sem("x_added")
        u_done = sem("u_done")
        u_copied = sem("u_copied")
        u_in_ring = sem("u_in_ring")
        z_done = sem("z_done")
        state_done = sem("state_done")
        state_scaled_done = sem("state_scaled_done")
        state_head = sem("state_head")
        states_out = sem("states_out")
        out_stored = sem("out_stored")

        PHASES = [(0, j) for j in range(BLOCKS)] + [(1, j) for j in range(BLOCKS)]
        PAIRS = (CH0 // 2, CH1 // 2)
        FIRST_TICK = 7

        def chunks_before(layer, j):
            return j * CH0 if layer == 0 else BLOCKS * CH0 + j * CH1

        def layer_of_piece(layer, j):
            return 0 if (layer, j) == (0, 0) else 1

        def tick_of(layer, j, k):
            pairs = (j * PAIRS[0] if layer == 0 else BLOCKS * PAIRS[0] + j * PAIRS[1]) + k
            tick = pairs - PAIRS[0] - FIRST_TICK
            return tick

        def has_tick(layer, j, k):
            return 0 <= tick_of(layer, j, k) < TICKS

        def loads(layer, j, k):
            if (layer, j) == (0, 0) and k < (SLOTS - EARLY) // 2:
                return EARLY // 2, 0
            if (layer, j) == (0, BLOCKS - 1) and k >= PAIRS[0] - PAIRS[1]:
                return SLOTS // 2, PAIRS[0] - PAIRS[1]
            return None

        SUM_COPY, SUM_TURN, NORM, NORM_TURN, INPUT_A, INPUT_B = 1, 2, 3, 4, 5, 6
        LOGITS, ROUTE, CW_TURN = 7, 8, 9
        LATE_LOGITS, LATE_ROUTE, LATE_CW_TURN = 4, 5, 6
        QUERY, DENOM, NUMER = 8, 9, 10
        O_TURN, OPEN = 0, 1
        STATES = 6
        EARLY_ROUTE = (2, 3, 4)

        def stages(phase, share):
            layer, j = PHASES[phase]
            own, other = Y[phase % 2], Y[(phase + 1) % 2]
            at = {}

            def put(k, name, *args):
                if name in share:
                    at.setdefault(k, []).append(lambda: share[name](*args))
            if layer == 0:
                put(O_TURN, "o_turn", j, own)
                put(OPEN, "project", j, own)
            else:
                put(OPEN, "open", own)
            if phase == 0:
                for i, k in enumerate(EARLY_ROUTE):
                    put(k, "route", i + 1)
                    put(k + 1, "cw_turn", i + 1, other[0])
            else:
                put(SUM_COPY, "sum_copy", phase - 1, other)
                put(SUM_TURN, "sum_turn", phase - 1, other)
                if phase <= BLOCKS:
                    put(NORM, "norm", phase - 1)
                    put(NORM_TURN, "norm_turn", BLOCKS + phase - 1, other)
                    put(INPUT_A, "inputs", phase - 1, 0, other)
                    put(INPUT_B, "inputs", phase - 1, 2, other)
                if phase < BLOCKS:
                    put(LOGITS, "logits", BLOCKS + phase - 1, other[0])
                    put(ROUTE, "route", BLOCKS + phase - 1)
                elif phase == BLOCKS + 1:
                    put(LATE_LOGITS, "logits", 2 * BLOCKS - 1, other[0])
                    put(LATE_ROUTE, "route", 2 * BLOCKS - 1)
                    put(LATE_CW_TURN, "cw_turn", 2 * BLOCKS - 1, other[1])
            if phase < BLOCKS - 1:
                put(QUERY, "query", phase + 1, other)
                put(DENOM, "denom", phase + 1, other)
            if 0 < phase < BLOCKS:
                put(CW_TURN, "cw_turn", BLOCKS + phase - 1, other[1])
            if phase < BLOCKS - 1:
                put(NUMER, "numer", phase + 1, other)
            if layer == 1:
                put(STATES, "states", j, own)
            if phase == 1:
                put(FIRST_TICK, "first_tick")
            elif 1 < phase < BLOCKS:
                put(FIRST_TICK, "more_inputs", phase)
            elif phase == BLOCKS + 1:
                put(0, "more_inputs", BLOCKS)
            return at

        def run_phase(eng, phase, pair, share):
            layer, j = PHASES[phase]
            at = stages(phase, share)
            kinds = [(has_tick(layer, j, k), loads(layer, j, k)) for k in range(PAIRS[layer])]
            cuts = [k for k in range(PAIRS[layer])
                    if k in (0, 1) or k in at or kinds[k] != kinds[k - 1] or tick_of(layer, j, k) == 1] + [PAIRS[layer]]
            for a, b in zip(cuts, cuts[1:]):
                for stage_ in at.get(a, []):
                    stage_()
                ticks, load = kinds[a]

                def run(k, ticks=ticks, load=load):
                    pair(k, tick_of(layer, j, k) if ticks else None, load[0] + (k - load[1]) if load else None)
                if b - a == 1:
                    run(a)
                else:
                    with eng.Fori(a, b) as k:
                        run(k)

        def after(eng, semaphore, value):
            if not isinstance(value, int) or value > 0:
                eng.wait_ge(semaphore, value)

        def states_ready(t):
            return 2 * (t // STEPS) + (1 if t % STEPS < HALF else 2)

        def head_cols(b, h):
            return slice((b * 2 + h) * (P // HEAD), (b * 2 + h + 1) * (P // HEAD))

        block = ctx.enter_context(nc.Block())

        @block.sync
        def _(sp):
            def load_x(j):
                sp.dma_start(xres[:, j, :, :], x[:, P * j:P * j + P, :].rearrange("b t d -> t b d"))\
                  .then_inc(x_loaded[j], 16)

            def load_early(s):
                sp.dma_start(early[:, s * PIECE:(s + 1) * PIECE], weights[s, :, :]).then_inc(early_loaded[s], 16)

            load_x(0)
            sp.dma_start(cst[:, :], consts).then_inc(consts_loaded, 16)
            sp.dma_start(vec[:, :], vectors).then_inc(consts_loaded, 16)
            load_x(1)
            for s in reversed(range(CHUNK0)):
                load_early(s)
            load_x(2)
            load_x(3)
            for s in range(CHUNK0, EARLY):
                load_early(s)
            for a in range(2):
                sp.dma_start(stage[:, a, :], weights[EARLY + a, :, :]).then_inc(stage_loaded[a], 16)
            with sp.Fori(EARLY // 2 + 1, (SLOTS + CH1) // 2) as r:
                for a in range(2):
                    sp.wait_ge(pieces_split, 2 * r + a - 1)
                    sp.dma_start(stage[:, a, :], weights[DS(2 * r + a, 1), :, :].rearrange("o p n -> (o p) n"))\
                      .then_inc(stage_loaded[a], 16)
            for j in range(BLOCKS):
                for half in range(2):
                    sp.wait_ge(x_added, 2 * (BLOCKS + j) + half + 1)
                    sp.dma_start(out[2 * half:2 * half + 2, P * j:P * j + P, :].rearrange("b t d -> t b d"),
                                 xres[:, j, 2 * half:2 * half + 2, :]).then_inc(out_stored, 16)
            sp.wait_ge(out_stored, 16 * 2 * BLOCKS)

        @block.tensor
        def _(pe):
            def weight(slot, part, off):
                return W[:, DS(slot, 1), part, off:off + P].rearrange("p o n -> p (o n)")

            PRODUCTS = ((0, 0), (0, 1), (1, 0))

            def split_product(bank_, terms, start=True, stop=True):
                n, count = 0, len(PRODUCTS) * len(terms)
                for w, act in terms:
                    for wp, ap in PRODUCTS:
                        last = nc.tensor.matmul(bank_, w(wp), act(ap), start=start and n == 0,
                                                stop=stop and n == count - 1)
                        n += 1
                return last

            def norm_turn(i, pair):
                pe.wait_ge(xn_done, BATCH * (i + 1))
                for b in range(BATCH):
                    for kd in range(KD):
                        last = nc.tensor.transpose(pair[kd][:, b * P:(b + 1) * P], xn[:, b, kd * P:(kd + 1) * P], ident)
                last.then_inc(xn_turned, 1)

            def logits(r, bank_):
                j, experts = r % BLOCKS, (E0, E1)[r // BLOCKS]
                off = 2 * DIM + (r // BLOCKS) * KD * E0
                pe.wait_ge(xtail_done, KD * (r + 1))
                if r >= BLOCKS:
                    pe.wait_ge(u_copied, KH * (j + 1))
                if r == 2 * BLOCKS - 1:
                    pe.wait_ge(x_added, 2 * (BLOCKS + 1))
                for b in range(BATCH):
                    n = 0
                    for kd in range(KD):
                        for xp in range(2):
                            for wp in range(2):
                                last = nc.tensor.matmul(
                                    bank_[:, b * experts:(b + 1) * experts], xT[:, j, kd, xp, b * P:(b + 1) * P],
                                    W[:, MISC, wp, off + kd * experts:off + (kd + 1) * experts],
                                    start=n == 0, stop=n == 4 * KD - 1)
                                n += 1
                last.then_inc(logits_done, 1)

            def cw_turn(r, bank_):
                pe.wait_ge(cw_done, r + 1)
                if 1 < r < BLOCKS:
                    pe.wait_ge(cwT_done, r)
                for b in range(BATCH):
                    last = nc.tensor.transpose(bank_[:, :].bitcast(bf16)[:, b * P:(b + 1) * P], cw3[:, b, :], identb[:, :])
                last.then_inc(cw_turned, 1)

            def query(j, pair):
                if j == 0:
                    pe.wait_ge(xtail_done, KD * BLOCKS)
                elif j == 1:
                    pe.wait_ge(cwT_done, BLOCKS)
                else:
                    pe.wait_ge(u_copied, KH * (j - 1))
                    pe.wait_ge(shifted_done, BLOCKS + j - 1)
                for h in range(2):
                    split_product(pair[h][:, :], [
                        (lambda p_, kd=kd: W[:, QKV + kd, p_, h * P:(h + 1) * P],
                         lambda p_, kd=kd: xT[:, j, kd, p_, :]) for kd in range(KD)]).then_inc(q_done, 1)

            def denom(j, pair):
                pe.wait_ge(q_copied, 2 * (j + 1))
                for b in range(BATCH):
                    for h in range(2):
                        last = nc.tensor.matmul(pair[0][:, head_cols(b, h)], qT[h][:, b * P:(b + 1) * P], KS[:, b, h, :],
                                                start=True, stop=True)
                last.then_inc(den_done, 1)

            def numer(j, pair):
                pe.wait_ge(rden_done, j + 1)
                if j >= 2:
                    pe.wait_ge(cwT_done, BLOCKS + j - 1)
                for b in range(BATCH):
                    for h in range(2):
                        at = (b % 2) * DIM + h * P
                        last = nc.tensor.matmul(pair[b // 2][:, at:at + P], qT[h][:, b * P:(b + 1) * P], BD[:, b, h, :],
                                                start=True, stop=True)
                    if b % 2:
                        last.then_inc(num_done, 1)

            def o_turn(j, pair):
                pe.wait_ge(o_done, 2 * (j + 1))
                if j == 0:
                    pe.wait_ge(cwT_done, 1)
                for h in range(2):
                    for b in range(BATCH):
                        last = nc.tensor.transpose(pair[h][:, b * P:(b + 1) * P], otok[:, b, h * P:(h + 1) * P], ident)
                    last.then_inc(o_turned, 1)

            def project(j, pair):
                pe.wait_ge(otail_done, 2 * (j + 1))
                for dh in range(KD):
                    split_product(pair[dh][:, :], [
                        (lambda p_, h=h: W[:, MISC, p_, h * DIM + dh * P:h * DIM + (dh + 1) * P],
                         lambda p_, h=h: oT[:, h, p_, :]) for h in range(2)], stop=False)

            def open_sum(pair):
                for dh in range(KD):
                    nc.tensor.matmul(pair[dh][:, :], zeros[:, 0:P], zeros[:, :], start=True, stop=False)

            def states(j, pair):
                pe.wait_ge(states_out, states_ready(P * (j + 1)))
                for dh in range(KD):
                    def w_out(c, dh=dh):
                        slot, off = (REC + c, HIDDEN) if c < 2 else (REC + 2, (c - 2) * DIM)
                        return lambda p_: W[:, slot, p_, off + dh * P:off + (dh + 1) * P]
                    split_product(pair[dh][:, :], [
                        (w_out(c), lambda p_, c=c: US16[:, BATCH * c:BATCH * (c + 1), P * j + 1:P * j + P + 1, p_])
                        for c in range(KH)], start=False, stop=False)

            def sum_turn(phase, pair):
                pe.wait_ge(y_copied, KD * (phase + 1))
                for half in range(2):
                    for b in range(2):
                        for dh in range(KD):
                            at = b * DIM + dh * P
                            last = nc.tensor.transpose(pair[half][:, at:at + P],
                                                       yT[dh][:, (2 * half + b) * P:(2 * half + b + 1) * P], ident)
                    last.then_inc(y_turned, 1)

            def inputs(j, c0, pair):
                pe.wait_ge(xtail_done, KD * (BLOCKS + j + 1))
                if c0:
                    pe.wait_ge(u_copied, KH * j + c0)
                if j == 0:
                    pe.wait_ge(pieces_split, SLOTS)
                for c in range(c0, c0 + 2):
                    split_product(pair[c - c0][:, :], [
                        (lambda p_, kd=kd: W[:, REC + kd, p_, c * P:(c + 1) * P],
                         lambda p_, kd=kd: xT[:, j, kd, p_, :]) for kd in range(KD)]).then_inc(u_done, 1)

            share = {"o_turn": o_turn, "project": project, "open": open_sum, "cw_turn": cw_turn,
                     "sum_turn": sum_turn, "norm_turn": norm_turn, "inputs": inputs, "logits": logits,
                     "query": query, "denom": denom, "numer": numer, "states": states}

            def keys_values(j, b):
                t = BATCH * j + b
                after(pe, kv_copied, t - 1)
                split_product(U[b % 2][:, :], [
                    (lambda p_, kd=kd: xT[:, j, kd, p_, b * P:(b + 1) * P],
                     lambda p_, kd=kd: W[:, QKV + kd, p_, DIM:3 * DIM]) for kd in range(KD)]).then_inc(kv_done, 1)

            def add_keys_values(j, b):
                pe.wait_ge(kv_copied, BATCH * j + b + 1)
                for h in range(2):
                    last = nc.tensor.matmul(kvsum[2 * b + h], kr[b % 2][:, h * P:(h + 1) * P], vx[b % 2][:, h, :],
                                            start=False, stop=j == BLOCKS - 1, skip_group_check=True)
                return last

            pe.wait_ge(zeros_made, 1)
            for bank_ in Y[0] + [G]:
                nc.tensor.matmul(bank_[:, :], zeros[:, 0:P], zeros[:, :], start=True, stop=False, skip_group_check=True)
            pe.wait_ge(consts_loaded, 32)
            norm_turn(0, Y[1])
            pe.wait_ge(pieces_split, CHUNK0)
            before = None
            for j in range(BLOCKS):
                after(pe, shifted_done, j)
                logits(j, C)
                for b in range(BATCH):
                    if b == 2 and j + 1 < BLOCKS:
                        norm_turn(j + 1, Y[1])
                    keys_values(j, b)
                    if before:
                        add_keys_values(*before)
                    before = (j, b)
            add_keys_values(*before).then_inc(kvsum_done, 1)
            query(0, Y[1])
            pe.wait_ge(kvsum_masked, 2 * 2 * BATCH)
            denom(0, Y[1])
            cw_turn(0, Y[0][0])
            numer(0, Y[1])

            def gate_up(layer, j, c, a):
                n = chunks_before(layer, j) + c
                slot = CHUNK0 + c
                if (layer, j) == (0, 0):
                    pe.wait_ge(pieces_split, c + CHUNK0 + 1)

                def product(bank_, off):
                    return split_product(bank_[:, :], [
                        (lambda p_, kd=kd: weight(slot, p_, off + kd * P),
                         lambda p_, kd=kd: xT[:, j, kd, p_, :]) for kd in range(KD)])
                after(pe, silu_done, n)
                product(G, 0).then_inc(gate_done, 1)
                after(pe, gated_done, n - 1)
                product(U[a], KD * P).then_inc(up_done, 1)
                after(pe, h_done, n)
                nc.tensor.matmul(C[:, :], sel[:, DS(c, 1), :].rearrange("p o n -> p (o n)"), cwT[:, layer, j, :],
                                 start=True, stop=True).then_inc(spread_done, 1)

            def down(phase, c, a, stop=False):
                layer, j = PHASES[phase]
                pe.wait_ge(htail_done, chunks_before(layer, j) + c + 1)
                act = (hh, hl)
                for dh in range(KD):
                    last = split_product(Y[phase % 2][dh][:, :], [
                        (lambda p_: weight(CHUNK0 + c, p_, 2 * KD * P + dh * P), lambda p_: act[p_][:, a, :])],
                        start=False, stop=stop)
                last.then_inc(down_done, 1)

            def last_down(phase, a):
                down(phase, CHUNKS[PHASES[phase][0]] - 2 + a, a, stop=a == 1)

            for phase, (layer, j) in enumerate(PHASES):
                if phase == 0:
                    pe.wait_ge(sel_made, 6)
                    pe.wait_ge(shifted_done, BLOCKS)
                if layer == 1:
                    pe.wait_ge(pieces_split, SLOTS + CH1)
                pe.wait_ge(cwT_done, phase + 1)

                def pair(k, tick, piece):
                    for a in range(2):
                        gate_up(layer, j, 2 * k + a, a)
                        if not isinstance(k, int) or k:
                            down(phase, 2 * k + a - 2, a)
                        elif phase:
                            last_down(phase - 1, a)
                run_phase(pe, phase, pair, share)
            for a in range(2):
                last_down(len(PHASES) - 1, a)
            sum_turn(len(PHASES) - 1, Y[(len(PHASES) - 1) % 2])

        @block.scalar
        def _(act):
            def split_head(slot, src):
                nc.scalar.activation(W[:, DS(slot, 1), 0, :].rearrange("p o n -> p (o n)"), src, ACT.Copy,
                                     scale=W_SCALE).then_inc(heads_split, 1)

            def split_early(s):
                act.wait_ge(early_loaded[s], 16)
                split_head(s, early[:, s * PIECE:(s + 1) * PIECE])

            def split_staged(layer, r, a):
                act.wait_ge(stage_loaded[a], 16 * (r - EARLY // 2 + 1))
                if layer == 0:
                    split_head(2 * r + a, stage[:, a, :])
                else:
                    act.wait_ge(down_done, (BLOCKS - 1) * CH0 + 2 * r + a - SLOTS + 1)
                    split_head(2 * r + a - SLOTS + CHUNK0, stage[:, a, :])

            def norm_turn(i, pair):
                act.wait_ge(xn_turned, i + 1)
                for kd in range(KD):
                    nc.scalar.activation(xT[:, i % BLOCKS, kd, 0, :], pair[kd][:, :], ACT.Copy).then_inc(xhead_done, 1)

            def logits(r, bank_):
                act.wait_ge(shifted_done, r + 1)
                g = gexp[:, r % BLOCKS, :, 0:(E0, E1)[r // BLOCKS]]
                nc.scalar.activation(g, g, ACT.Exp, scale=1.0 / W_SCALE).then_inc(exp_done, 1)

            def cw_turn(r, bank_):
                act.wait_ge(cw_turned, r + 1)
                nc.scalar.activation(cwT[:, r // BLOCKS, r % BLOCKS, :], bank_[:, :].bitcast(bf16)[:, 0:COLS], ACT.Copy)\
                  .then_inc(cwT_done, 1)

            def query(j, pair):
                for h in range(2):
                    act.wait_ge(q_done, 2 * j + h + 1)
                    nc.scalar.activation(qT[h], pair[h][:, :], ACT.Relu, scale=1.0 / W_SCALE).then_inc(q_copied, 1)

            def o_turn(j, pair):
                for h in range(2):
                    act.wait_ge(o_turned, 2 * j + h + 1)
                    nc.scalar.activation(oT[:, h, 0, :], pair[h][:, :], ACT.Copy, scale=H_SCALE).then_inc(ohead_done, 1)

            def sum_copy(phase, pair):
                layer, j = PHASES[phase]
                act.wait_ge(down_done, chunks_before(layer, j) + CHUNKS[layer])
                for dh in range(KD):
                    bias = vec[:, 3 * KH + layer * KD + dh:3 * KH + layer * KD + dh + 1]
                    nc.scalar.activation(yT[dh], pair[dh][:, :], ACT.Identity, bias=bias, scale=Y_DESCALE)\
                      .then_inc(y_copied, 1)

            def inputs(j, c0, pair):
                for c in range(c0, c0 + 2):
                    act.wait_ge(u_done, KH * j + c + 1)
                    nc.scalar.activation(US[:, BATCH * c:BATCH * (c + 1), P * j:P * (j + 1)],
                                         pair[c - c0][:, :].rearrange("p (b t) -> p b t", b=BATCH), ACT.Identity,
                                         bias=ubias[:, c:c + 1], scale=1.0 / W_SCALE).then_inc(u_copied, 1)

            def first_tick():
                nc.scalar.activation(ring[:, 0, 0::2], gam[:, 0::2], ACT.Copy).then_inc(state_done, 1)

            share = {"norm_turn": norm_turn, "logits": logits, "cw_turn": cw_turn, "query": query, "o_turn": o_turn,
                     "sum_copy": sum_copy, "inputs": inputs, "first_tick": first_tick}

            norm_turn(0, Y[1])
            for s in reversed(range(CHUNK0)):
                split_early(s)
            act.wait_ge(ones_made, 1)
            for j in range(BLOCKS):
                logits(j, C)
                for b in range(BATCH):
                    if b == 2 and j + 1 < BLOCKS:
                        norm_turn(j + 1, Y[1])
                    act.wait_ge(kv_done, BATCH * j + b + 1)
                    nc.scalar.activation(kr[b % 2], U[b % 2][:, 0:DIM], ACT.Relu, scale=1.0 / W_SCALE)
                    nc.scalar.activation(vx[b % 2][:, :, 0:P], U[b % 2][:, DIM:2 * DIM].rearrange("p (h e) -> p h e", h=2),
                                         ACT.Copy, scale=1.0 / W_SCALE).then_inc(kv_copied, 1)
            query(0, Y[1])
            cw_turn(0, Y[0][0])
            for s in range(CHUNK0, EARLY):
                split_early(s)

            def silu(n, a):
                act.wait_ge(gate_done, n + 1)
                after(act, gated_done, n - 1)
                nc.scalar.activation(sg[a], G[:, :], ACT.Silu, scale=1.0 / W_SCALE).then_inc(silu_done, 1)

            def h_head(n, a):
                act.wait_ge(h_done, n + 1)
                nc.scalar.activation(hh[:, a, :], h32[a], ACT.Copy).then_inc(hhead_done, 1)

            def step(tick, i):
                if tick is None:
                    return
                if i == HALF - 1:
                    after(act, states_out, 2 * tick)
                if i == STEPS - 1:
                    act.wait_ge(states_out, 2 * tick + 1)
                act.wait_ge(z_done, STEPS * tick + i + 1)
                nc.scalar.activation(ring[:, (i + 1) % STEPS, 0::2], zbuf[:, 1::2], ACT.Tanh).then_inc(state_done, 1)

            for phase, (layer, j) in enumerate(PHASES):
                def pair(k, tick, piece):
                    n = chunks_before(layer, j) + 2 * k
                    step(tick, 0)
                    silu(n, 0)
                    step(tick, 1)
                    step(tick, 2)
                    if phase or not isinstance(k, int) or k:
                        h_head(n - 1, 1)
                    step(tick, 3)
                    step(tick, 4)
                    step(tick, 5)
                    silu(n + 1, 1)
                    step(tick, 6)
                    step(tick, 7)
                    h_head(n, 0)
                    step(tick, 8)
                    step(tick, 9)
                    if piece is not None:
                        for a in range(2):
                            split_staged(layer_of_piece(layer, j), piece, a)
                run_phase(act, phase, pair, share)
            n = chunks_before(*PHASES[-1]) + CHUNKS[1]
            act.wait_ge(down_done, n - 2)
            h_head(n - 1, 1)
            sum_copy(len(PHASES) - 1, Y[(len(PHASES) - 1) % 2])

        @block.vector
        def _(dve):
            ordered = [0]

            def mark(ins):
                ordered[0] += 1
                return ins.then_inc(dve_order, 1)

            def settle():
                dve.wait_ge(dve_order, ordered[0])

            def norm_stats(j):
                settle()
                for b in range(BATCH):
                    mark(nc.vector.bn_stats(stats[:, b, :], xres[:, j, b, :]))
                settle()
                for b in range(BATCH):
                    mark(nc.vector.bn_aggr(mv[:, b, :], stats[:, b, :]))
                settle()

            def norm(j):
                mark(nc.vector.tensor_scalar(var[:, :], mv[:, :, 1], EPS_NORM, None, ALU.add))
                settle()
                mark(nc.vector.tensor_scalar(guess[:, :], var[:, :].bitcast(i32), 1, None, ALU.logical_shift_right))
                mark(nc.vector.tensor_scalar(half_var[:, :], var[:, :], -0.5, None, ALU.mult))
                settle()
                mark(nc.vector.tensor_scalar(rstd[:, :].bitcast(i32), guess[:, :], -1.0, float(0x5F3759DF), ALU.mult, ALU.add))
                settle()
                for _ in range(3):
                    mark(nc.vector.tensor_tensor(var[:, :], rstd[:, :], rstd[:, :], ALU.mult))
                    settle()
                    mark(nc.vector.tensor_tensor(var[:, :], var[:, :], half_var[:, :], ALU.mult))
                    settle()
                    mark(nc.vector.scalar_tensor_tensor(out=rstd[:, :], in0=var[:, :], scalar=1.5, in1=rstd[:, :],
                                                        op0=ALU.add, op1=ALU.mult))
                    settle()
                for b in range(BATCH):
                    nc.vector.tensor_scalar(xn[:, b, :], xres[:, j, b, :], mv[:, b, 0:1], rstd[:, b:b + 1],
                                            ALU.subtract, ALU.mult).then_inc(xn_done, 1)

            def norm_turn(i, pair):
                for kd in range(KD):
                    dve.wait_ge(xhead_done, KD * i + kd + 1)
                    nc.vector.tensor_tensor(xT[:, i % BLOCKS, kd, 1, :], pair[kd][:, :], xT[:, i % BLOCKS, kd, 0, :],
                                            ALU.subtract).then_inc(xtail_done, 1)

            def split_tail(slot, count, src):
                dve.wait_ge(heads_split, count + 1)
                dst = W[:, DS(slot, 1), :, :].rearrange("p o h n -> p (o h) n")
                nc.vector.scalar_tensor_tensor(out=dst[:, 1, :], in0=src, scalar=W_SCALE, in1=dst[:, 0, :],
                                               op0=ALU.mult, op1=ALU.subtract).then_inc(pieces_split, 1)

            def logits(r, bank_):
                E = (E0, E1)[r // BLOCKS]
                lg = bank_[:, 0:BATCH * E].rearrange("p (b e) -> p b e", e=E)
                dve.wait_ge(logits_done, r + 1)
                settle()
                if r:
                    dve.wait_ge(shifted_done, r)
                mark(nc.vector.tensor_reduce(gmax[:, :], lg, AX.X, ALU.max))
                settle()
                nc.vector.tensor_tensor(gexp[:, r % BLOCKS, :, 0:E], lg, gmax[:, :].unsqueeze(2).broadcast_to([P, BATCH, E]),
                                        ALU.subtract).then_inc(shifted_done, 1)

            def route(r):
                layer = r // BLOCKS
                E, K = ((E0, K0), (E1, K1))[layer]
                g = gexp[:, r % BLOCKS, :, 0:E]
                rest = 8 - K
                spread = [P, BATCH, E]
                p = gprob[:, :, 0:E]
                dve.wait_ge(exp_done, r + 1)
                settle()
                if r:
                    dve.wait_ge(cw_turned, r)
                    dve.wait_ge(cw_done, r)
                if r in (0, BLOCKS):
                    mark(nc.vector.memset(cw3[:, :, :], 0.0))
                    mark(nc.vector.memset(gprob[:, :, E:E + rest], -1.0))
                mark(nc.vector.tensor_reduce(gsum[:, 0, :], g, AX.X, ALU.add))
                settle()
                mark(nc.vector.reciprocal(gsum[:, 1, :], gsum[:, 0, :]))
                settle()
                mark(nc.vector.tensor_tensor(p, g, gsum[:, 1, :].unsqueeze(2).broadcast_to(spread), ALU.mult))
                settle()
                for b in range(BATCH):
                    mark(nc.vector.max(gtop[:, b, :], gprob[:, b, 0:E]))
                settle()
                mark(nc.vector.memset(gtop[:, :, K:8], -1.0))
                settle()
                for b in range(BATCH):
                    mark(nc.vector.match_replace(out=grest[:, b, 0:E + rest], in_to_replace=gtop[:, b, :],
                                                 in_values=gprob[:, b, 0:E + rest], imm_value=0.0))
                settle()
                cw = grest[:, :, 0:E]
                mark(nc.vector.tensor_tensor(cw, p, cw, ALU.subtract))
                settle()
                if layer == 1:
                    mark(nc.vector.tensor_reduce(gsum[:, 0, :], cw, AX.X, ALU.add))
                    settle()
                    mark(nc.vector.tensor_scalar(gsum[:, 0, :], gsum[:, 0, :], EPS_TOPK, None, ALU.add))
                    settle()
                    mark(nc.vector.reciprocal(gsum[:, 1, :], gsum[:, 0, :]))
                    settle()
                    mark(nc.vector.tensor_tensor(cw, cw, gsum[:, 1, :].unsqueeze(2).broadcast_to(spread), ALU.mult))
                    if r == BLOCKS:
                        mark(nc.vector.memset(cw3[:, :, E:E + SHARED], 1.0))
                    settle()
                for part, at in enumerate(SPLIT_AT):
                    piece = cw3[:, :, at:at + E]
                    if part == 2:
                        nc.vector.tensor_copy(piece, cw).then_inc(cw_done, 1)
                        break
                    mark(nc.vector.tensor_copy(piece, cw))
                    settle()
                    mark(nc.vector.tensor_tensor(cw, cw, piece, ALU.subtract))
                    settle()

            def denom(j, pair):
                dve.wait_ge(den_done, j + 1)
                settle()
                if j:
                    dve.wait_ge(o_done, 2 * j)
                mark(nc.vector.tensor_scalar(rden[:, :], pair[0][:, 0:BATCH * DIM // HEAD], EPS_ATTN, None, ALU.add))
                settle()
                nc.vector.reciprocal(rden[:, :], rden[:, :]).then_inc(rden_done, 1)

            def numer(j, pair):
                dve.wait_ge(rden_done, j + 1)
                heads = 2 * DIM // HEAD
                for half in range(2):
                    dve.wait_ge(num_done, 2 * j + half + 1)
                    nc.vector.tensor_tensor(
                        otok[:, 2 * half:2 * half + 2, :].rearrange("p b (h e) -> p (b h) e", e=HEAD),
                        pair[half][:, :].rearrange("p (h e) -> p h e", e=HEAD),
                        rden[:, half * heads:(half + 1) * heads].unsqueeze(2).broadcast_to([P, heads, HEAD]),
                        ALU.mult).then_inc(o_done, 1)

            def o_turn(j, pair):
                for h in range(2):
                    dve.wait_ge(ohead_done, 2 * j + h + 1)
                    nc.vector.scalar_tensor_tensor(out=oT[:, h, 1, :], in0=pair[h][:, :], scalar=H_SCALE, in1=oT[:, h, 0, :],
                                                   op0=ALU.mult, op1=ALU.subtract).then_inc(otail_done, 1)

            def sum_turn(phase, pair):
                j = PHASES[phase][1]
                for half in range(2):
                    dve.wait_ge(y_turned, 2 * phase + half + 1)
                    nc.vector.tensor_tensor(xres[:, j, 2 * half:2 * half + 2, :], xres[:, j, 2 * half:2 * half + 2, :],
                                            pair[half][:, :].rearrange("p (b d) -> p b d", b=2), ALU.add)\
                      .then_inc(x_added, 1)
                if phase < BLOCKS:
                    dve.wait_ge(x_added, 2 * (phase + 1))
                    norm_stats(j)

            share = {"logits": logits, "route": route, "denom": denom, "numer": numer, "o_turn": o_turn,
                     "sum_turn": sum_turn, "norm": norm, "norm_turn": norm_turn}

            mark(nc.vector.memset(gam[:, :], 0.0))
            for n in range(2):
                mark(nc.vector.memset(vx[n][:, :, P:SUM], 1.0))
            settle()
            dve.wait_ge(consts_loaded, 32)
            for b in range(BATCH):
                mark(nc.vector.tensor_copy(gam[:, :].rearrange("p (c b two) -> p c b two", b=BATCH, two=2)[:, :, b, 1],
                                           vec[:, 0:KH]))
            mark(nc.vector.tensor_tensor(ubias[:, :], vec[:, KH:2 * KH], vec[:, 2 * KH:3 * KH], ALU.add))
            settle()
            nc.vector.tensor_copy(identb[:, :], ident).then_inc(ones_made, 1)
            for j in range(BLOCKS):
                dve.wait_ge(x_loaded[j], 16)
                norm_stats(j)
                after(dve, xn_turned, j)
                norm(j)
                if j == 0:
                    norm_turn(0, Y[1])
                    for s in reversed(range(CHUNK0)):
                        split_tail(s, CHUNK0 - 1 - s, early[:, s * PIECE:(s + 1) * PIECE])
                else:
                    logits(j - 1, C)
                    norm_turn(j, Y[1])
            logits(BLOCKS - 1, C)
            route(0)
            dve.wait_ge(kvsum_done, 1)
            for b in range(BATCH):
                for h in range(2):
                    kv = kvsum[2 * b + h]
                    nc.vector.tensor_tensor(KS[:, b, h, :], mask[:, ::HEAD], kv[:, P:SUM].broadcast_to([P, P // HEAD]),
                                            ALU.mult).then_inc(kvsum_masked, 1)
                    nc.vector.tensor_tensor(BD[:, b, h, :], mask, kv[:, 0:P], ALU.mult).then_inc(kvsum_masked, 1)
            denom(0, Y[1])
            numer(0, Y[1])
            for s in range(CHUNK0, EARLY):
                split_tail(s, s, early[:, s * PIECE:(s + 1) * PIECE])
            dve.wait_ge(pieces_split, EARLY)
            mark(nc.vector.memset(US[:, :, SEQ:SLOTS_T + 8], 0.0))

            def step(tick, i):
                if tick is None:
                    return
                if i % HALF == 0:
                    dve.wait_ge(u_in_ring, 2 * tick + i // HALF + 1)
                dve.wait_ge(state_done, STEPS * tick + i + 1)
                nc.vector.tensor_tensor_scan(zbuf[:, :], gam[:, :], ring[:, i, :], 0.0, ALU.mult, ALU.add)\
                  .then_inc(z_done, 1)

            def gated(n, a):
                dve.wait_ge(silu_done, n + 1)
                dve.wait_ge(up_done, n + 1)
                after(dve, htail_done, n - 1)
                nc.vector.tensor_tensor(h32[a], sg[a], U[a][:, :], ALU.mult).then_inc(gated_done, 1)

            def routed(n, a):
                dve.wait_ge(gated_done, n + 1)
                dve.wait_ge(spread_done, n + 1)
                nc.vector.tensor_tensor(h32[a], h32[a], C[:, :], ALU.mult).then_inc(h_done, 1)

            for phase, (layer, j) in enumerate(PHASES):
                def pair(k, tick, piece):
                    n = chunks_before(layer, j) + 2 * k
                    step(tick, 0)
                    gated(n, 0)
                    step(tick, 1)
                    step(tick, 2)
                    routed(n, 0)
                    step(tick, 3)
                    step(tick, 4)
                    step(tick, 5)
                    gated(n + 1, 1)
                    step(tick, 6)
                    step(tick, 7)
                    routed(n + 1, 1)
                    step(tick, 8)
                    step(tick, 9)
                    if piece is not None:
                        for a in range(2):
                            slot = piece * 2 + a - (SLOTS - CHUNK0 if layer_of_piece(layer, j) else 0)
                            split_tail(slot, 2 * piece + a, stage[:, a, :])
                run_phase(dve, phase, pair, share)
            sum_turn(len(PHASES) - 1, Y[(len(PHASES) - 1) % 2])

        @block.gpsimd
        def _(pool):
            nc.gpsimd.memset(zeros[:, :], 0.0).then_inc(zeros_made, 1)
            nc.gpsimd.memset(h_scale[:, :, :], H_SCALE).then_inc(pool_order, 1)
            nc.gpsimd.memset(sel[:, :, :], 0.0).then_inc(pool_order, 1)
            pool.wait_ge(pool_order, 2)
            for r, at in enumerate(SPLIT_AT):
                rows = sel[at:at + E0, :, :]
                nc.gpsimd.memset(rows, 1.0).then_inc(pool_order, 1)
                pool.wait_ge(pool_order, 3 + r)
                nc.gpsimd.affine_select(out=rows, in_=rows, compare_op=ALU.is_ge, fill=0.0, base=0,
                                        pattern=[[P, CH0], [1, P]], channel_multiplier=-FE).then_inc(sel_made, 1)
                pool.wait_ge(sel_made, 2 * r + 1)
                nc.gpsimd.affine_select(out=rows, in_=rows, compare_op=ALU.is_ge, fill=0.0, base=FE - 1,
                                        pattern=[[-P, CH0], [-1, P]], channel_multiplier=FE).then_inc(sel_made, 1)

            def h_tail(n, a):
                pool.wait_ge(hhead_done, n + 1)
                nc.gpsimd.tensor_tensor(hl[:, a, :], h32[a], hh[:, a, :], ALU.subtract).then_inc(htail_done, 1)

            def rows_of(half, which):
                return ring[:, half * HALF:(half + 1) * HALF, which::2].rearrange("p r l -> p l r")

            def take_u(tick, half):
                nc.gpsimd.tensor_copy(rows_of(half, 1), US[:, :, DS(STEPS * tick + half * HALF, HALF)]).then_inc(u_in_ring, 1)

            def keep_states(tick, half):
                span = US16[:, :, DS(STEPS * tick + half * HALF, HALF), :]
                kept = state_scaled[:, half, :, :]
                nc.gpsimd.tensor_tensor(kept, rows_of(half, 0), h_scale[:, :, :], ALU.mult).then_inc(state_scaled_done, 1)
                pool.wait_ge(state_scaled_done, 2 * tick + half + 1)
                nc.gpsimd.tensor_copy(span[:, :, :, 0], kept).then_inc(state_head, 1)
                pool.wait_ge(state_head, 2 * tick + half + 1)
                nc.gpsimd.tensor_tensor(span[:, :, :, 1], kept, span[:, :, :, 0], ALU.subtract)\
                  .then_inc(states_out, 1)

            def first_tick():
                pool.wait_ge(u_copied, KH)
                take_u(0, 0)

            def more_inputs(blocks):
                pool.wait_ge(u_copied, KH * blocks)

            share = {"first_tick": first_tick, "more_inputs": more_inputs}

            for phase, (layer, j) in enumerate(PHASES):
                def pair(k, tick, piece):
                    n = chunks_before(layer, j) + 2 * k
                    if tick is not None:
                        pool.wait_ge(state_done, STEPS * tick + 1)
                        if not isinstance(tick, int) or tick:
                            keep_states(tick - 1, 1)
                        take_u(tick, 1)
                    if phase or not isinstance(k, int) or k:
                        h_tail(n - 1, 1)
                    if tick is not None:
                        pool.wait_ge(state_done, STEPS * tick + HALF + 1)
                        keep_states(tick, 0)
                        take_u(tick + 1, 0)
                    h_tail(n, 0)
                run_phase(pool, phase, pair, share)
            h_tail(chunks_before(*PHASES[-1]) + CHUNKS[1] - 1, 1)


def kernel(**inputs):
    import numpy as np
    import concourse.bacc as bacc
    from concourse.bass_utils import run_bass_kernel_spmd

    a = {n: np.asarray(v) for n, v in inputs.items()}

    def over_rows(m):
        t = np.ascontiguousarray(m.T)
        return t.reshape(t.shape[0] // P, P, t.shape[1])

    def chunk_pieces(gates, ups, downs, chunks):
        units = chunks * P
        padded = []
        for m in (gates, ups, downs):
            q = np.zeros((units, DIM), m.dtype)
            q[:m.shape[0]] = m
            padded.append(q)
        res = np.zeros((chunks, P, PIECE), gates.dtype)
        for c in range(chunks):
            rows = slice(c * P, (c + 1) * P)
            for i, m in enumerate(padded[:2]):
                t = over_rows(m[rows])
                for kd in range(KD):
                    res[c, :, (i * KD + kd) * P:(i * KD + kd + 1) * P] = t[kd]
            res[c, :, 2 * KD * P:] = padded[2][rows]
        return res

    def rows_of_down(w):
        return np.swapaxes(w, 1, 2).reshape(-1, DIM)

    qkv = over_rows(a["L0_attn_w_qkv"])
    proj = over_rows(a["L0_attn_w_proj"])
    gate0, gate1 = over_rows(a["L0_ffn_gate_w"]), over_rows(a["L1_ffn_gate_weight"])
    w_in, w_out = over_rows(a["L1_attn_W_in"]), over_rows(a["L1_attn_W_out"])
    misc = np.zeros((P, PIECE), qkv.dtype)
    body = np.concatenate([proj[0], proj[1], gate0[0], gate0[1], gate1[0], gate1[1]], axis=1)
    misc[:, :body.shape[1]] = body
    last = np.zeros((P, PIECE), qkv.dtype)
    last[:, :2 * DIM] = np.concatenate([w_out[2], w_out[3]], axis=1)
    moe0 = chunk_pieces(a["L0_ffn_w_gate"].reshape(-1, DIM), a["L0_ffn_w_up"].reshape(-1, DIM),
                        rows_of_down(a["L0_ffn_w_down"]), CH0)
    moe1 = chunk_pieces(np.concatenate([a["L1_ffn_w_gate"].reshape(-1, DIM), a["L1_ffn_sw_gate"]]),
                        np.concatenate([a["L1_ffn_w_up"].reshape(-1, DIM), a["L1_ffn_sw_up"]]),
                        np.concatenate([rows_of_down(a["L1_ffn_w_down"]), a["L1_ffn_sw_down"].T]), CH1)
    rec = [np.concatenate([w_in[0], w_out[0]], axis=1), np.concatenate([w_in[1], w_out[1]], axis=1), last]
    weights = np.ascontiguousarray(np.concatenate([np.stack([qkv[0], qkv[1], misc]), moe0, np.stack(rec), moe1]))

    def column(v):
        return v.reshape(-1, P).T

    vectors = np.ascontiguousarray(np.concatenate([column(a[n]) for n in (
        "L1_attn_gamma", "L1_attn_beta", "L1_attn_b_in", "L0_attn_b_proj", "L1_attn_b_out")], axis=1))
    consts = np.concatenate([np.eye(P), np.kron(np.eye(P // HEAD), np.ones((HEAD, HEAD)))], axis=1).astype(np.float32)
    x = np.ascontiguousarray(a["L0_attn_x"])

    nc = bacc.Bacc("TRN2", target_bir_lowering=False, num_devices=1)
    f32 = mybir.dt.float32
    arrays = {"x": x, "weights": weights, "consts": consts, "vectors": vectors}
    aps = [nc.dram_tensor(n, v.shape, f32, kind="ExternalInput").ap() for n, v in arrays.items()]
    out = nc.dram_tensor("out", x.shape, f32, kind="ExternalOutput").ap()
    build(nc, *aps, out)
    r = run_bass_kernel_spmd(nc, [arrays], core_ids=[0])
    return r.results[0]["out"]
```

```python
import concourse.bass as bass
from concourse import mybir
from contextlib import ExitStack


P = 128
BATCH, SEQ, DIM = 4, 512, 256
KD = DIM // P
BLOCKS = SEQ // P
COLS = BATCH * P
HEAD = 32
EPS_ATTN = 1e-15
EPS_NORM = 1e-5
EPS_TOPK = 1e-20
FE = 176
E0, K0 = 16, 6
E1, K1, SHARED = 8, 2, 2
CH0 = E0 * FE // P
CH1 = -(-(E1 + SHARED) * FE // P)
CHUNKS = (CH0, CH1)
UNITS0, UNITS1 = FE // CH0, FE // (CH1 - 1)
UNITS_LAST = FE - (CH1 - 1) * UNITS1
UNITS_SHARED = P - E1 * UNITS1
SHARED_LAST = SHARED * FE - (CH1 - 1) * UNITS_SHARED
assert UNITS0 * CH0 == FE and E1 * UNITS_LAST + SHARED_LAST <= min(P, E0 * UNITS_LAST) and E0 * UNITS1 >= P
HIDDEN = 512
KH = HIDDEN // P
LANES = KH * BATCH
W_SCALE = 64.0
H_SCALE = 64.0
Y_DESCALE = 1.0 / (W_SCALE * H_SCALE)

PIECE = 768
QKV, MISC, CHUNK0, REC = 0, 2, 3, 3 + CH0
SLOTS = REC + 3
EARLY = 8
WARM_UP = 16
STEPS = 10
HALF = STEPS // 2
TICKS = -(-SEQ // STEPS)
SLOTS_T = TICKS * STEPS
SPLIT_AT = (0, 32, 64)


def build(nc, x, weights, consts, vectors, out):
    f32, f16, bf16, i32 = mybir.dt.float32, mybir.dt.float16, mybir.dt.bfloat16, mybir.dt.int32
    ALU, ACT, AX = mybir.AluOpType, mybir.ActivationFunctionType, mybir.AxisListType
    DS = bass.ds

    ctx = ExitStack()
    with ctx:
        def sb(name, shape, dt=f32):
            return ctx.enter_context(nc.sbuf_tensor(name, shape, dt))

        def sem(name):
            return ctx.enter_context(nc.semaphore(name))

        W = sb("W", [P, SLOTS, 2, PIECE], f16)
        stage = sb("stage", [P, 2, PIECE])
        xres = sb("xres", [P, BLOCKS, BATCH, DIM])
        xT = sb("xT", [P, BLOCKS, KD, 2, COLS], f16)
        US = sb("US", [P, LANES, SLOTS_T + 8])
        ring = sb("ring", [P, STEPS, 2 * LANES])
        state_scaled = sb("state_scaled", [P, 2, LANES, HALF])
        h_scale = sb("h_scale", [P, LANES, HALF])
        zbuf = sb("zbuf", [P, 2 * LANES])
        gam = sb("gam", [P, 2 * LANES])
        scr = sb("scr", [P, 8, COLS])
        hh = sb("hh", [P, 2, COLS], f16)
        hl = sb("hl", [P, 2, COLS], f16)
        BD = sb("BD", [P, BATCH, 2, P])
        KS = sb("KS", [P, BATCH, 2, P // HEAD])
        rden = sb("rden", [P, BATCH * DIM // HEAD])
        zeros = sb("zeros", [P, COLS], bf16)
        sel = sb("sel", [P, 3, P], bf16)
        CS = sb("CS", [P, 3, COLS])
        cwT = sb("cwT", [P, 2, BLOCKS, COLS], bf16)
        cst = sb("cst", [P, 2 * P])
        identb = sb("identb", [P, P], bf16)
        vec = sb("vec", [P, 3 * KH + 2 * KD])
        ubias = sb("ubias", [P, KH])
        unused = sb("unused", [P, 1])
        stats = sb("stats", [P, BATCH, 6])
        mv = sb("mv", [P, BATCH, 2])
        rstd = sb("rstd", [P, BATCH])
        var = sb("var", [P, BATCH])
        half_var = sb("half_var", [P, BATCH])
        guess = sb("guess", [P, BATCH], i32)
        gmax = sb("gmax", [P, BATCH])
        gsum = sb("gsum", [P, 2, BATCH])
        gexp = sb("gexp", [P, BLOCKS, BATCH, E0])
        gprob = sb("gprob", [P, BATCH, E0 + 8])
        grest = sb("grest", [P, BATCH, E0 + 8])
        gtop = sb("gtop", [P, BATCH, 8])
        cw3 = sb("cw3", [P, BATCH, P], bf16)
        ident, mask = cst[:, 0:P], cst[:, P:2 * P]

        def scratch(n, dt=f32):
            return scr[:, n:n + 2, :].rearrange("p a n -> p (a n)").bitcast(dt)
        sg = [scr[:, 0, :], scr[:, 1, :]]
        h32 = [scr[:, 2, :], scr[:, 3, :]]
        kr = [scr[:, 0, 0:DIM], scr[:, 1, 0:DIM]]
        vx = [scr[:, 2 + n, 0:2 * (P + 1)].rearrange("p (h e) -> p h e", h=2)
              for n in range(2)]
        xn = scratch(4).rearrange("p (b d) -> p b d", b=BATCH)
        qT = [scr[:, 4, :], scr[:, 5, :]]
        oT = scratch(4, f16).rearrange("p (h two n) -> p h two n", h=2, two=2)
        yT = [scr[:, 6, :], scr[:, 7, :]]
        otok = scratch(6).rearrange("p (b d) -> p b d", b=BATCH)
        early = US[:, :, :].rearrange("p a b -> p (a b)")
        US16 = US[:, :, :].rearrange("p a b -> p (a b)").bitcast(f16).rearrange(
            "p (a b two) -> p a b two", a=LANES, two=2)

        def bank(name):
            return ctx.enter_context(nc.psum_tensor(name, [P, 512], f32))
        G = bank("G")
        U = [bank("U0"), bank("U1")]
        C = bank("C")
        Y = [[bank("Y00"), bank("Y01")], [bank("Y10"), bank("Y11")]]
        SUM = P + 1
        IN_G = 2 * BATCH - 6
        kvsum = [(Y[0] + [G])[g // 3][:, (g % 3) * SUM:(g % 3 + 1) * SUM] for g in range(2 * BATCH)]

        x_loaded = [sem(f"x_loaded{j}") for j in range(BLOCKS)]
        x0_rest_loaded = sem("x0_rest_loaded")
        consts_loaded = sem("consts_loaded")
        early_loaded = [sem(f"early_loaded{s}") for s in range(EARLY)]
        stage_loaded = [sem("stage_loaded0"), sem("stage_loaded1")]
        heads_split = sem("heads_split")
        pieces_split = sem("pieces_split")
        early_scaled = sem("early_scaled")
        sel_made = sem("sel_made")
        zeros_made = sem("zeros_made")
        ones_made = sem("ones_made")
        consts_made = sem("consts_made")
        dve_order = sem("dve_order")
        pool_order = sem("pool_order")
        xn_done = sem("xn_done")
        xn_turned = sem("xn_turned")
        xhead_done = sem("xhead_done")
        xtail_done = sem("xtail_done")
        logits_done = sem("logits_done")
        shifted_done = sem("shifted_done")
        exp_done = sem("exp_done")
        cw_done = sem("cw_done")
        cw_turned = sem("cw_turned")
        cwT_done = sem("cwT_done")
        kv_done = sem("kv_done")
        kv_copied = sem("kv_copied")
        kvsum_done = sem("kvsum_done")
        kvsum_masked = sem("kvsum_masked")
        q_done = sem("q_done")
        q_copied = sem("q_copied")
        den_done = sem("den_done")
        rden_done = sem("rden_done")
        num_done = sem("num_done")
        o_done = sem("o_done")
        o_turned = sem("o_turned")
        ohead_done = sem("ohead_done")
        otail_done = sem("otail_done")
        gate_done = sem("gate_done")
        up_done = sem("up_done")
        spread_done = sem("spread_done")
        spread_copied = sem("spread_copied")
        silu_done = sem("silu_done")
        gated_done = sem("gated_done")
        h_done = sem("h_done")
        hhead_done = sem("hhead_done")
        htail_done = sem("htail_done")
        down_done = sem("down_done")
        y_copied = sem("y_copied")
        y_turned = sem("y_turned")
        x_added = sem("x_added")
        u_done = sem("u_done")
        u_copied = sem("u_copied")
        u_in_ring = sem("u_in_ring")
        z_done = sem("z_done")
        state_done = sem("state_done")
        state_scaled_done = sem("state_scaled_done")
        state_head = sem("state_head")
        states_out = sem("states_out")
        out_stored = sem("out_stored")

        CONSTS_MADE = BATCH + 3

        PHASES = [(0, j) for j in range(BLOCKS)] + [(1, j) for j in range(BLOCKS)]
        PAIRS = (CH0 // 2, CH1 // 2)
        FIRST_TICK = 7

        def chunks_before(layer, j):
            return j * CH0 if layer == 0 else BLOCKS * CH0 + j * CH1

        def tick_of(layer, j, k):
            pairs = (j * PAIRS[0] if layer == 0 else BLOCKS * PAIRS[0] + j * PAIRS[1]) + k
            return pairs - PAIRS[0] - FIRST_TICK

        def has_tick(layer, j, k):
            return 0 <= tick_of(layer, j, k) < TICKS

        def loads(layer, j, k):
            late = PAIRS[0] - 1
            if (layer, j) == (0, 0) and k < (SLOTS - EARLY) // 2:
                return 2, EARLY, 0
            if (layer, j) == (0, BLOCKS - 1) and k >= 1:
                return 1, SLOTS, 1
            if (layer, j) == (1, 0) and k < CH1 - late:
                return 1, SLOTS + late, 0
            return None

        SUM_COPY, SUM_TURN, NORM, NORM_TURN, INPUT_A, INPUT_B = 1, 2, 2, 4, 5, 6
        LOGITS = 5
        EXP = {BLOCKS: (2, 5), BLOCKS + 1: (2, 5), BLOCKS + 2: (4, 5), BLOCKS + 3: (4, 5)}
        ROUTE = {BLOCKS: (2, 6), BLOCKS + 1: (2, 8), BLOCKS + 2: (4, 6), BLOCKS + 3: (5, 1)}
        CW_TURN = {BLOCKS: (2, 8), BLOCKS + 1: (2, 10), BLOCKS + 2: (5, 1), BLOCKS + 3: (5, 4)}
        QUERY, DENOM, NUMER = 7, 8, 9
        O_TURN, PROJECT = 0, 2
        FIRST_DENOM, FIRST_NUMER, FIRST_O_TURN, FIRST_PROJECT = 1, 2, 3, 4
        EARLY_ROUTE = (2, 4, 6)
        SPREAD = (9, 5)
        SPREAD_LAST = 3
        STATES = 6

        def stages(phase):
            layer, j = PHASES[phase]
            own, other = Y[phase % 2], Y[(phase + 1) % 2]
            front = [[] for _ in range(PAIRS[layer])]
            woven = [[] for _ in range(PAIRS[layer])]
            if phase == 0:
                front[FIRST_DENOM].append(("denom", (0, other)))
                front[FIRST_NUMER].append(("numer", (0, other)))
                front[FIRST_O_TURN].append(("o_turn", (0, other)))
                front[FIRST_PROJECT].append(("project", (0, own)))
                for i, k in enumerate(EARLY_ROUTE):
                    woven[k].append(("route", (i + 1, 0)))
                    front[k + 2].append(("cw_turn", (i + 1, C)))
            elif layer == 0:
                front[O_TURN].append(("o_turn", (j, own)))
            if phase:
                front[SUM_COPY].append(("sum_copy", (phase - 1, other)))
                front[SUM_TURN].append(("sum_turn", (phase - 1, other)))
            if 1 <= phase < BLOCKS:
                front[PROJECT].append(("project", (j, own)))
            if 1 <= phase <= BLOCKS:
                r = BLOCKS + phase - 1
                woven[NORM].append(("norm", (phase - 1, 0)))
                woven[NORM + 1].append(("norm", (phase - 1, STEPS)))
                front[NORM_TURN].append(("norm_turn", (r, other)))
                front[LOGITS].append(("logits", (r, other[1])))
                front[INPUT_A].append(("inputs", (phase - 1, 0, other)))
                front[INPUT_B].append(("inputs", (phase - 1, 2, other)))
            if phase < BLOCKS - 1:
                front[QUERY].append(("query", (phase + 1, other)))
                front[DENOM].append(("denom", (phase + 1, other)))
            for r in range(BLOCKS, 2 * BLOCKS):
                if EXP[r][0] == phase:
                    front[EXP[r][1]].append(("exp", (r,)))
                if ROUTE[r][0] == phase:
                    woven[ROUTE[r][1]].append(("route", (r, 0)))
                if CW_TURN[r][0] == phase:
                    front[CW_TURN[r][1]].append(("cw_turn", (r, C)))
            if phase < BLOCKS - 1:
                front[NUMER].append(("numer", (phase + 1, other)))
            if layer == 1:
                front[SPREAD_LAST].append(("spread", (phase, True)))
                if phase + 1 < len(PHASES):
                    front[STATES].append(("states", (j, own)))
            if phase + 1 < len(PHASES):
                front[SPREAD[layer]].append(("spread", (phase + 1, False)))
            if phase == 1:
                front[FIRST_TICK].append(("first_tick", ()))
            elif 1 < phase < BLOCKS:
                front[FIRST_TICK].append(("more_inputs", (phase,)))
            elif phase == BLOCKS + 1:
                front[0].append(("more_inputs", (BLOCKS,)))
            return front, woven

        def run_phase(eng, phase, pair, share):
            layer, j = PHASES[phase]
            front, woven = ([[s for s in at if s[0] in share] for at in table] for table in stages(phase))
            pairs = range(PAIRS[layer])
            kinds = [(has_tick(layer, j, k), loads(layer, j, k)) for k in pairs]

            def cut(k):
                return (k in (0, 1) or front[k] or woven[k] or woven[k - 1] or kinds[k] != kinds[k - 1]
                        or tick_of(layer, j, k) == 1 or (kinds[k][1] and kinds[k][1][0] == 1))
            cuts = [k for k in pairs if cut(k)] + [PAIRS[layer]]
            for a, b in zip(cuts, cuts[1:]):
                for name, args in front[a]:
                    share[name](*args)
                ticks, load = kinds[a]

                def run(k, ticks=ticks, load=load, woven=woven[a]):
                    pieces = [load[0] * (k - load[2]) + load[1] + i for i in range(load[0])] if load else []
                    pair(k, tick_of(layer, j, k) if ticks else None, pieces, woven)
                if b - a == 1:
                    run(a)
                else:
                    with eng.Fori(a, b) as k:
                        run(k)

        def after(eng, semaphore, value):
            if not isinstance(value, int) or value > 0:
                eng.wait_ge(semaphore, value)

        def slot_of(piece):
            return piece - SLOTS + CHUNK0 if isinstance(piece, int) and piece >= SLOTS else piece

        def spreads(phase, last):
            return phase + 1 + max(0, phase - BLOCKS) + last

        uses_of_C = [("cw_turn", 0), ("spread", (0, False))]
        for phase in range(len(PHASES)):
            for at in stages(phase)[0]:
                uses_of_C += [(name, args[0] if name == "cw_turn" else args) for name, args in at
                              if name in ("cw_turn", "spread")]

        def turned_before(phase, last):
            return [name for name, _ in uses_of_C[:uses_of_C.index(("spread", (phase, last)))]].count("cw_turn")

        def spread_before(r):
            return [name for name, _ in uses_of_C[:uses_of_C.index(("cw_turn", r))]].count("spread")

        def out_bias(layer, dh):
            at = 3 * KH + layer * KD + dh
            return vec[:, at:at + 1]

        def spread_slot(phase, last):
            return CS[:, 2 if last else phase % 2, :]

        def states_ready(t):
            return 2 * (t // STEPS) + (1 if t % STEPS < HALF else 2)

        def head_cols(b, h):
            return slice((b * 2 + h) * (P // HEAD), (b * 2 + h + 1) * (P // HEAD))

        block = ctx.enter_context(nc.Block())

        @block.sync
        def _(sp):
            def load_x(j):
                sp.dma_start(xres[:, j, :, :], x[:, P * j:P * j + P, :].rearrange("b t d -> t b d"))\
                  .then_inc(x_loaded[j], 16)

            def load_early(s):
                sp.dma_start(early[:, s * PIECE:(s + 1) * PIECE], weights[s, :, :]).then_inc(early_loaded[s], 16)

            for half in range(2):
                pair = slice(2 * half, 2 * half + 2)
                sp.dma_start(xres[:, 0, pair, :], x[pair, 0:P, :].rearrange("b t d -> t b d"))\
                  .then_inc((x_loaded[0], x0_rest_loaded)[half], 16)
            sp.dma_start(cst[:, :], consts).then_inc(consts_loaded, 16)
            sp.dma_start(vec[:, :], vectors).then_inc(consts_loaded, 16)
            for s in reversed(range(CHUNK0)):
                load_early(s)
            load_x(1)
            load_x(2)
            load_x(3)
            for s in range(CHUNK0, EARLY):
                load_early(s)
            for a in range(2):
                sp.dma_start(stage[:, a, :], weights[EARLY + a, :, :]).then_inc(stage_loaded[a], 16)
            with sp.Fori(EARLY // 2 + 1, (SLOTS + CH1) // 2) as r:
                for a in range(2):
                    sp.wait_ge(pieces_split, 2 * r + a - 1)
                    sp.dma_start(stage[:, a, :], weights[DS(2 * r + a, 1), :, :].rearrange("o p n -> (o p) n"))\
                      .then_inc(stage_loaded[a], 16)
            for j in range(BLOCKS):
                for half in range(2):
                    sp.wait_ge(x_added, 2 * (BLOCKS + j) + half + 1)
                    sp.dma_start(out[2 * half:2 * half + 2, P * j:P * j + P, :].rearrange("b t d -> t b d"),
                                 xres[:, j, 2 * half:2 * half + 2, :]).then_inc(out_stored, 16)
            sp.wait_ge(out_stored, 16 * 2 * BLOCKS)

        @block.tensor
        def _(pe):
            def weight(slot, part, off):
                return W[:, DS(slot, 1), part, off:off + P].rearrange("p o n -> p (o n)")

            PRODUCTS = ((0, 0), (0, 1), (1, 0))

            def split_product(bank_, terms, start=True, stop=True):
                n, count = 0, len(PRODUCTS) * len(terms)
                for w, act in terms:
                    for wp, ap in PRODUCTS:
                        last = nc.tensor.matmul(bank_, w(wp), act(ap), start=start and n == 0,
                                                stop=stop and n == count - 1)
                        n += 1
                return last

            def norm_turn(i, pair):
                for b in range(BATCH):
                    pe.wait_ge(xn_done, BATCH * i + b + 1)
                    for kd in range(KD):
                        last = nc.tensor.transpose(pair[kd][:, b * P:(b + 1) * P], xn[:, b, kd * P:(kd + 1) * P], ident)
                last.then_inc(xn_turned, 1)

            def logits(r, bank_):
                j, experts = r % BLOCKS, (E0, E1)[r // BLOCKS]
                off = 2 * DIM + (r // BLOCKS) * KD * E0
                pe.wait_ge(xtail_done, KD * (r + 1))
                for b in range(BATCH):
                    n = 0
                    for kd in range(KD):
                        for xp in range(2):
                            for wp in range(2):
                                last = nc.tensor.matmul(
                                    bank_[:, b * experts:(b + 1) * experts], xT[:, j, kd, xp, b * P:(b + 1) * P],
                                    W[:, MISC, wp, off + kd * experts:off + (kd + 1) * experts],
                                    start=n == 0, stop=n == 4 * KD - 1)
                                n += 1
                last.then_inc(logits_done, 1)

            def cw_turn(r, bank_):
                pe.wait_ge(cw_done, r + 1)
                if r == 0:
                    pe.wait_ge(consts_made, CONSTS_MADE)
                pe.wait_ge(shifted_done, BLOCKS)
                after(pe, cwT_done, r)
                after(pe, spread_copied, spread_before(r))
                for b in range(BATCH):
                    last = nc.tensor.transpose(bank_[:, :].bitcast(bf16)[:, b * P:(b + 1) * P],
                                               cw3[:, b, :], identb[:, :])
                last.then_inc(cw_turned, 1)

            def query(j, pair):
                if j == 0:
                    pe.wait_ge(xtail_done, KD * BLOCKS)
                elif j > 1:
                    pe.wait_ge(u_copied, KH * (j - 1))
                    pe.wait_ge(shifted_done, BLOCKS + j - 1)
                for h in range(2):
                    split_product(pair[h][:, :], [
                        (lambda p_, kd=kd: W[:, QKV + kd, p_, h * P:(h + 1) * P],
                         lambda p_, kd=kd: xT[:, j, kd, p_, :]) for kd in range(KD)]).then_inc(q_done, 1)

            def denom(j, pair):
                pe.wait_ge(q_copied, 2 * (j + 1))
                if j == 0:
                    pe.wait_ge(kvsum_masked, 2 * 2 * BATCH)
                for b in range(BATCH):
                    for h in range(2):
                        last = nc.tensor.matmul(pair[0][:, head_cols(b, h)], qT[h][:, b * P:(b + 1) * P],
                                                KS[:, b, h, :],
                                                start=True, stop=True)
                last.then_inc(den_done, 1)

            def numer(j, pair):
                pe.wait_ge(rden_done, j + 1)
                for b in range(BATCH):
                    for h in range(2):
                        at = (b % 2) * DIM + h * P
                        last = nc.tensor.matmul(pair[b // 2][:, at:at + P], qT[h][:, b * P:(b + 1) * P], BD[:, b, h, :],
                                                start=True, stop=True)
                    if b % 2:
                        last.then_inc(num_done, 1)

            def o_turn(j, pair):
                pe.wait_ge(o_done, 2 * (j + 1))
                for h in range(2):
                    for b in range(BATCH):
                        last = nc.tensor.transpose(pair[h][:, b * P:(b + 1) * P], otok[:, b, h * P:(h + 1) * P], ident)
                    last.then_inc(o_turned, 1)

            def project(j, pair):
                pe.wait_ge(otail_done, 2 * (j + 1))
                for dh in range(KD):
                    split_product(pair[dh][:, :], [
                        (lambda p_, h=h: W[:, MISC, p_, h * DIM + dh * P:h * DIM + (dh + 1) * P],
                         lambda p_, h=h: oT[:, h, p_, :]) for h in range(2)], start=False, stop=False)

            def states(j, pair):
                pe.wait_ge(states_out, states_ready(P * (j + 1)))
                for dh in range(KD):
                    def w_out(c, dh=dh):
                        slot, off = (REC + c, HIDDEN) if c < 2 else (REC + 2, (c - 2) * DIM)
                        return lambda p_: W[:, slot, p_, off + dh * P:off + (dh + 1) * P]
                    split_product(pair[dh][:, :], [
                        (w_out(c), lambda p_, c=c: US16[:, BATCH * c:BATCH * (c + 1), P * j + 1:P * j + P + 1, p_])
                        for c in range(KH)], start=False, stop=False)

            def sum_turn(phase, pair):
                pe.wait_ge(y_copied, KD * (phase + 1))
                for half in range(2):
                    for b in range(2):
                        for dh in range(KD):
                            at = b * DIM + dh * P
                            last = nc.tensor.transpose(pair[half][:, at:at + P],
                                                       yT[dh][:, (2 * half + b) * P:(2 * half + b + 1) * P], ident)
                    last.then_inc(y_turned, 1)

            def inputs(j, c0, pair):
                pe.wait_ge(xtail_done, KD * (BLOCKS + j + 1))
                if c0:
                    pe.wait_ge(u_copied, KH * j + c0)
                if j == 0:
                    pe.wait_ge(pieces_split, SLOTS)
                for c in range(c0, c0 + 2):
                    if c == 1:
                        pe.wait_ge(shifted_done, BLOCKS + j + 1)
                    split_product(pair[c - c0][:, :], [
                        (lambda p_, kd=kd: W[:, REC + kd, p_, c * P:(c + 1) * P],
                         lambda p_, kd=kd: xT[:, j, kd, p_, :]) for kd in range(KD)]).then_inc(u_done, 1)

            def spread(phase, last):
                pe.wait_ge(cwT_done, turned_before(phase, last))
                after(pe, spread_copied, spreads(phase, last) - 1)
                nc.tensor.matmul(C[:, :], sel[:, 2 if last else phase // BLOCKS, :],
                                 cwT[:, phase // BLOCKS, phase % BLOCKS, :], start=True, stop=True)\
                  .then_inc(spread_done, 1)

            share = {"spread": spread, "o_turn": o_turn, "project": project, "cw_turn": cw_turn,
                     "sum_turn": sum_turn, "norm_turn": norm_turn, "inputs": inputs, "logits": logits,
                     "query": query, "denom": denom, "numer": numer, "states": states}

            def keys_values(j, b):
                t = BATCH * j + b
                after(pe, kv_copied, t - 1)
                pe.wait_ge(xhead_done, KD * (j + 1))
                n = 0
                for xp, wp in PRODUCTS:
                    if b == 0 and xp == 1:
                        pe.wait_ge(xtail_done, KD * (j + 1))
                    for kd in range(KD):
                        last = nc.tensor.matmul(U[b % 2][:, :], xT[:, j, kd, xp, b * P:(b + 1) * P],
                                                W[:, QKV + kd, wp, DIM:3 * DIM], start=n == 0, stop=n == KD * 3 - 1)
                        n += 1
                last.then_inc(kv_done, 1)

            def add_keys_values(j, b):
                pe.wait_ge(kv_copied, BATCH * j + b + 1)
                for h in range(2):
                    last = nc.tensor.matmul(kvsum[2 * b + h], kr[b % 2][:, h * P:(h + 1) * P], vx[b % 2][:, h, :],
                                            start=False, stop=j == BLOCKS - 1, skip_group_check=True)
                return last

            pe.wait_ge(zeros_made, 1)
            for bank_ in Y[0] + [G]:
                nc.tensor.matmul(bank_[:, :], zeros[:, 0:P], zeros[:, :], start=True, stop=False, skip_group_check=True)
            for _ in range(WARM_UP):
                nc.tensor.matmul(U[0][:, :], zeros[:, 0:P], zeros[:, :], start=True, stop=True)
            pe.wait_ge(consts_loaded, 32)
            norm_turn(0, Y[1])
            pe.wait_ge(pieces_split, CHUNK0)
            before = None
            for j in range(BLOCKS):
                for b in range(BATCH):
                    if b == 1:
                        after(pe, shifted_done, j)
                        logits(j, C)
                    if b == (2 if j else 3) and j + 1 < BLOCKS:
                        norm_turn(j + 1, Y[1])
                    keys_values(j, b)
                    if before:
                        add_keys_values(*before)
                    before = (j, b)
            add_keys_values(*before).then_inc(kvsum_done, 1)
            cw_turn(0, C)
            query(0, Y[1])
            pe.wait_ge(sel_made, 2 * 3 * len(SPLIT_AT))
            spread(0, False)

            def gate_up(layer, j, c, a):
                n = chunks_before(layer, j) + c
                slot = CHUNK0 + c
                if (layer, j) == (0, 0):
                    pe.wait_ge(pieces_split, c + CHUNK0 + 1)
                if (layer, j) == (1, 0):
                    pe.wait_ge(pieces_split, c + SLOTS + 1)

                def product(bank_, off):
                    return split_product(bank_[:, :], [
                        (lambda p_, kd=kd: weight(slot, p_, off + kd * P),
                         lambda p_, kd=kd: xT[:, j, kd, p_, :]) for kd in range(KD)])
                if (layer, j) == (0, 0):
                    pe.wait_ge(kvsum_masked, 2 * IN_G)
                after(pe, silu_done, n)
                product(G, 0).then_inc(gate_done, 1)
                after(pe, gated_done, n - 1)
                product(U[a], KD * P).then_inc(up_done, 1)

            def down(phase, c, a, start=False, stop=False):
                layer, j = PHASES[phase]
                pe.wait_ge(htail_done, chunks_before(layer, j) + c + 1)
                act = (hh, hl)
                for dh in range(KD):
                    last = split_product(Y[phase % 2][dh][:, :], [
                        (lambda p_: weight(CHUNK0 + c, p_, 2 * KD * P + dh * P), lambda p_: act[p_][:, a, :])],
                        start=start, stop=stop)
                last.then_inc(down_done, 1)

            def last_down(phase, a):
                down(phase, CHUNKS[PHASES[phase][0]] - 2 + a, a, stop=a == 1)

            for phase, (layer, j) in enumerate(PHASES):
                def pair(k, tick, pieces, woven):
                    for a in range(2):
                        gate_up(layer, j, 2 * k + a, a)
                        if not isinstance(k, int) or k:
                            first = isinstance(k, int) and (k, a) == (1, 0)
                            down(phase, 2 * k + a - 2, a, start=first)
                        elif phase:
                            last_down(phase - 1, a)
                run_phase(pe, phase, pair, share)
            last_down(len(PHASES) - 1, 0)
            states(BLOCKS - 1, Y[(len(PHASES) - 1) % 2])
            last_down(len(PHASES) - 1, 1)
            sum_turn(len(PHASES) - 1, Y[(len(PHASES) - 1) % 2])

        @block.scalar
        def _(act):
            def split_head(slot, src):
                nc.scalar.activation(W[:, DS(slot, 1), 0, :].rearrange("p o n -> p (o n)"), src, ACT.Copy,
                                     scale=W_SCALE).then_inc(heads_split, 1)

            def split_early(s):
                act.wait_ge(early_loaded[s], 16)
                split_head(s, early[:, s * PIECE:(s + 1) * PIECE])

            def split_staged(piece, a):
                act.wait_ge(stage_loaded[a], 8 * (piece - EARLY - a) + 16)
                if isinstance(piece, int) and piece >= SLOTS:
                    act.wait_ge(down_done, (BLOCKS - 1) * CH0 + piece - SLOTS + 1)
                split_head(slot_of(piece), stage[:, a, :])

            def norm_turn(i, pair):
                act.wait_ge(xn_turned, i + 1)
                for kd in range(KD):
                    nc.scalar.activation(xT[:, i % BLOCKS, kd, 0, :], pair[kd][:, :], ACT.Copy).then_inc(xhead_done, 1)

            def exp(r):
                act.wait_ge(shifted_done, r + 1)
                g = gexp[:, r % BLOCKS, :, 0:(E0, E1)[r // BLOCKS]]
                nc.scalar.activation(g, g, ACT.Exp, scale=1.0 / W_SCALE).then_inc(exp_done, 1)

            def cw_turn(r, bank_):
                act.wait_ge(cw_turned, r + 1)
                nc.scalar.activation(cwT[:, r // BLOCKS, r % BLOCKS, :], bank_[:, :].bitcast(bf16)[:, 0:COLS],
                                     ACT.Copy)\
                  .then_inc(cwT_done, 1)

            def query(j, pair):
                for h in range(2):
                    act.wait_ge(q_done, 2 * j + h + 1)
                    nc.scalar.activation(qT[h], pair[h][:, :], ACT.Relu, scale=1.0 / W_SCALE).then_inc(q_copied, 1)

            def o_turn(j, pair):
                for h in range(2):
                    act.wait_ge(o_turned, 2 * j + h + 1)
                    nc.scalar.activation(oT[:, h, 0, :], pair[h][:, :], ACT.Copy, scale=H_SCALE).then_inc(ohead_done, 1)

            def sum_copy(phase, pair):
                layer, j = PHASES[phase]
                act.wait_ge(down_done, chunks_before(layer, j) + CHUNKS[layer])
                for dh in range(KD if phase + 1 < len(PHASES) else 1):
                    nc.scalar.activation(yT[dh], pair[dh][:, :], ACT.Identity, bias=out_bias(layer, dh),
                                         scale=Y_DESCALE)\
                      .then_inc(y_copied, 1)

            def inputs(j, c0, pair):
                for c in range(c0, c0 + 2):
                    act.wait_ge(u_done, KH * j + c + 1)
                    nc.scalar.activation(US[:, BATCH * c:BATCH * (c + 1), P * j:P * (j + 1)],
                                         pair[c - c0][:, :].rearrange("p (b t) -> p b t", b=BATCH), ACT.Identity,
                                         bias=ubias[:, c:c + 1], scale=1.0 / W_SCALE).then_inc(u_copied, 1)

            def first_tick():
                nc.scalar.activation(ring[:, 0, 0::2], gam[:, 0::2], ACT.Copy).then_inc(state_done, 1)

            def spread(phase, last):
                act.wait_ge(spread_done, spreads(phase, last))
                used = phase if last else phase - 1
                if used > 0:
                    act.wait_ge(h_done, chunks_before(*PHASES[used]))
                nc.scalar.activation(spread_slot(phase, last), C[:, :], ACT.Copy).then_inc(spread_copied, 1)

            share = {"spread": spread, "norm_turn": norm_turn, "exp": exp, "cw_turn": cw_turn, "query": query,
                     "o_turn": o_turn,
                     "sum_copy": sum_copy, "inputs": inputs, "first_tick": first_tick}

            for s in reversed(range(CHUNK0)):
                split_early(s)
            norm_turn(0, Y[1])
            act.wait_ge(ones_made, 2)
            for j in range(BLOCKS):
                for b in range(BATCH):
                    if b == (2 if j else 3) and j + 1 < BLOCKS:
                        norm_turn(j + 1, Y[1])
                    act.wait_ge(kv_done, BATCH * j + b + 1)
                    nc.scalar.activation(kr[b % 2], U[b % 2][:, 0:DIM], ACT.Relu, scale=1.0 / W_SCALE)
                    nc.scalar.activation(vx[b % 2][:, :, 0:P],
                                         U[b % 2][:, DIM:2 * DIM].rearrange("p (h e) -> p h e", h=2),
                                         ACT.Copy, scale=1.0 / W_SCALE).then_inc(kv_copied, 1)
                if j:
                    exp(j - 1)
                split_early(CHUNK0 + j)
            exp(BLOCKS - 1)
            act.wait_ge(consts_made, CONSTS_MADE)
            nc.scalar.activation(unused[:, :], ubias[:, 0:1], ACT.Silu)
            cw_turn(0, C)
            query(0, Y[1])
            spread(0, False)
            for s in range(CHUNK0 + BLOCKS, EARLY):
                split_early(s)

            def silu(n, a):
                act.wait_ge(gate_done, n + 1)
                after(act, gated_done, n - 1)
                nc.scalar.activation(sg[a], G[:, :], ACT.Silu, scale=1.0 / W_SCALE).then_inc(silu_done, 1)

            def h_head(n, a):
                act.wait_ge(h_done, n + 1)
                nc.scalar.activation(hh[:, a, :], h32[a], ACT.Copy).then_inc(hhead_done, 1)

            def step(tick, i):
                if tick is None:
                    return
                if i == HALF - 1:
                    after(act, states_out, 2 * tick)
                if i == STEPS - 1:
                    act.wait_ge(states_out, 2 * tick + 1)
                act.wait_ge(z_done, STEPS * tick + i + 1)
                nc.scalar.activation(ring[:, (i + 1) % STEPS, 0::2], zbuf[:, 1::2], ACT.Tanh).then_inc(state_done, 1)

            for phase, (layer, j) in enumerate(PHASES):
                def pair(k, tick, pieces, woven):
                    n = chunks_before(layer, j) + 2 * k
                    for a in range(2):
                        step(tick, HALF * a)
                        silu(n + a, a)
                        for i in range(1, HALF - 1):
                            step(tick, HALF * a + i)
                        if a or phase or not isinstance(k, int) or k:
                            h_head(n + a - 1, 1 - a)
                        step(tick, HALF * a + HALF - 1)
                    for a, piece in enumerate(pieces):
                        split_staged(piece, piece % 2 if len(pieces) == 1 else a)
                run_phase(act, phase, pair, share)
            n = chunks_before(*PHASES[-1]) + CHUNKS[1]
            act.wait_ge(down_done, n - 2)
            h_head(n - 1, 1)
            sum_copy(len(PHASES) - 1, Y[(len(PHASES) - 1) % 2])

        @block.vector
        def _(dve):
            ordered = [0]

            def mark(ins):
                ordered[0] += 1
                return ins.then_inc(dve_order, 1)

            def settle():
                dve.wait_ge(dve_order, ordered[0])

            def norm(j, part, weaving=True):
                if part in (0, 4, 5, 6, 7, 8, 9, 10, 11):
                    settle()
                if part < BATCH:
                    mark(nc.vector.bn_stats(stats[:, part, :], xres[:, j, part, :]))
                elif part == 4:
                    for b in range(BATCH):
                        mark(nc.vector.bn_aggr(mv[:, b, :], stats[:, b, :]))
                elif part == 5:
                    mark(nc.vector.tensor_scalar(var[:, :], mv[:, :, 1], EPS_NORM, None, ALU.add))
                elif part == 6:
                    mark(nc.vector.tensor_scalar(guess[:, :], var[:, :].bitcast(i32), 1, None, ALU.logical_shift_right))
                    mark(nc.vector.tensor_scalar(half_var[:, :], var[:, :], -0.5, None, ALU.mult))
                elif part == 7:
                    mark(nc.vector.tensor_scalar(rstd[:, :].bitcast(i32), guess[:, :], -1.0, float(0x5F3759DF),
                                                 ALU.mult, ALU.add))
                elif part < 11:
                    mark(nc.vector.tensor_tensor(var[:, :], rstd[:, :], rstd[:, :], ALU.mult))
                    settle()
                    mark(nc.vector.tensor_tensor(var[:, :], var[:, :], half_var[:, :], ALU.mult))
                    settle()
                    mark(nc.vector.scalar_tensor_tensor(out=rstd[:, :], in0=var[:, :], scalar=1.5, in1=rstd[:, :],
                                                        op0=ALU.add, op1=ALU.mult))
                elif part < 11 + BATCH:
                    b = part - 11
                    if weaving and b == 0:
                        dve.wait_ge(down_done, chunks_before(*PHASES[j + 1]) + 3)
                    nc.vector.tensor_scalar(xn[:, b, :], xres[:, j, b, :], mv[:, b, 0:1], rstd[:, b:b + 1],
                                            ALU.subtract, ALU.mult).then_inc(xn_done, 1)

            def norm_turn(i, pair):
                for kd in range(KD):
                    dve.wait_ge(xhead_done, KD * i + kd + 1)
                    nc.vector.tensor_tensor(xT[:, i % BLOCKS, kd, 1, :], pair[kd][:, :], xT[:, i % BLOCKS, kd, 0, :],
                                            ALU.subtract).then_inc(xtail_done, 1)

            def split_tail(slot, count, src):
                dve.wait_ge(heads_split, count + 1)
                dst = W[:, DS(slot, 1), :, :].rearrange("p o h n -> p (o h) n")
                nc.vector.scalar_tensor_tensor(out=dst[:, 1, :], in0=src, scalar=W_SCALE, in1=dst[:, 0, :],
                                               op0=ALU.mult, op1=ALU.subtract).then_inc(pieces_split, 1)

            def logits(r, bank_):
                E = (E0, E1)[r // BLOCKS]
                lg = bank_[:, 0:BATCH * E].rearrange("p (b e) -> p b e", e=E)
                dve.wait_ge(logits_done, r + 1)
                settle()
                if r:
                    dve.wait_ge(shifted_done, r)
                mark(nc.vector.tensor_reduce(gmax[:, :], lg, AX.X, ALU.max))
                settle()
                nc.vector.tensor_tensor(gexp[:, r % BLOCKS, :, 0:E], lg,
                                        gmax[:, :].unsqueeze(2).broadcast_to([P, BATCH, E]),
                                        ALU.subtract).then_inc(shifted_done, 1)

            def route(r, part):
                layer = r // BLOCKS
                E, K = ((E0, K0), (E1, K1))[layer]
                g = gexp[:, r % BLOCKS, :, 0:E]
                rest = 8 - K
                spread = [P, BATCH, E]
                p = gprob[:, :, 0:E]
                cw = grest[:, :, 0:E]

                def split_part(n):
                    piece = cw3[:, :, SPLIT_AT[n]:SPLIT_AT[n] + E]
                    if n == 2:
                        nc.vector.tensor_copy(piece, cw).then_inc(cw_done, 1)
                        return
                    mark(nc.vector.tensor_copy(piece, cw))
                    settle()
                    mark(nc.vector.tensor_tensor(cw, cw, piece, ALU.subtract))
                settle()
                if part == 0:
                    dve.wait_ge(exp_done, r + 1)
                    if r:
                        dve.wait_ge(cw_done, r)
                    if r in (0, BLOCKS):
                        mark(nc.vector.memset(gprob[:, :, E:E + rest], -1.0))
                    mark(nc.vector.tensor_reduce(gsum[:, 0, :], g, AX.X, ALU.add))
                elif part == 1:
                    mark(nc.vector.reciprocal(gsum[:, 1, :], gsum[:, 0, :]))
                    settle()
                    mark(nc.vector.tensor_tensor(p, g, gsum[:, 1, :].unsqueeze(2).broadcast_to(spread), ALU.mult))
                elif part == 2:
                    for b in range(BATCH):
                        mark(nc.vector.max(gtop[:, b, :], gprob[:, b, 0:E]))
                elif part == 3:
                    mark(nc.vector.memset(gtop[:, :, K:8], -1.0))
                elif part == 4:
                    for b in range(BATCH):
                        mark(nc.vector.match_replace(out=grest[:, b, 0:E + rest], in_to_replace=gtop[:, b, :],
                                                     in_values=gprob[:, b, 0:E + rest], imm_value=0.0))
                elif part == 5:
                    mark(nc.vector.tensor_tensor(cw, p, cw, ALU.subtract))
                    if r:
                        dve.wait_ge(cw_turned, r)
                    if r in (0, BLOCKS):
                        mark(nc.vector.memset(cw3[:, :, :], 0.0))
                elif part == 6 and layer == 1:
                    mark(nc.vector.tensor_reduce(gsum[:, 0, :], cw, AX.X, ALU.add))
                    settle()
                    mark(nc.vector.tensor_scalar(gsum[:, 0, :], gsum[:, 0, :], EPS_TOPK, None, ALU.add))
                elif part == 7 and layer == 1:
                    mark(nc.vector.reciprocal(gsum[:, 1, :], gsum[:, 0, :]))
                    settle()
                    mark(nc.vector.tensor_tensor(cw, cw, gsum[:, 1, :].unsqueeze(2).broadcast_to(spread), ALU.mult))
                    if r == BLOCKS:
                        mark(nc.vector.memset(cw3[:, :, E:E0], 1.0))
                elif part == 8:
                    split_part(0)
                elif part == 9:
                    split_part(1)
                    settle()
                    split_part(2)

            def denom(j, pair):
                dve.wait_ge(den_done, j + 1)
                settle()
                if j:
                    dve.wait_ge(o_done, 2 * j)
                mark(nc.vector.tensor_scalar(rden[:, :], pair[0][:, 0:BATCH * DIM // HEAD], EPS_ATTN, None, ALU.add))
                settle()
                nc.vector.reciprocal(rden[:, :], rden[:, :]).then_inc(rden_done, 1)

            def numer(j, pair):
                dve.wait_ge(rden_done, j + 1)
                heads = 2 * DIM // HEAD
                for half in range(2):
                    dve.wait_ge(num_done, 2 * j + half + 1)
                    nc.vector.tensor_tensor(
                        otok[:, 2 * half:2 * half + 2, :].rearrange("p b (h e) -> p (b h) e", e=HEAD),
                        pair[half][:, :].rearrange("p (h e) -> p h e", e=HEAD),
                        rden[:, half * heads:(half + 1) * heads].unsqueeze(2).broadcast_to([P, heads, HEAD]),
                        ALU.mult).then_inc(o_done, 1)

            def o_turn(j, pair):
                for h in range(2):
                    dve.wait_ge(ohead_done, 2 * j + h + 1)
                    nc.vector.scalar_tensor_tensor(out=oT[:, h, 1, :], in0=pair[h][:, :], scalar=H_SCALE,
                                                   in1=oT[:, h, 0, :],
                                                   op0=ALU.mult, op1=ALU.subtract).then_inc(otail_done, 1)

            def sum_turn(phase, pair):
                j = PHASES[phase][1]
                for half in range(2):
                    dve.wait_ge(y_turned, 2 * phase + half + 1)
                    nc.vector.tensor_tensor(xres[:, j, 2 * half:2 * half + 2, :], xres[:, j, 2 * half:2 * half + 2, :],
                                            pair[half][:, :].rearrange("p (b d) -> p b d", b=2), ALU.add)\
                      .then_inc(x_added, 1)
                if phase < BLOCKS:
                    dve.wait_ge(x_added, 2 * (phase + 1))

            share = {"logits": logits, "route": route, "denom": denom, "numer": numer, "o_turn": o_turn,
                     "sum_turn": sum_turn, "norm": norm, "norm_turn": norm_turn}

            def block_stats(j):
                dve.wait_ge(x_loaded[j], 16)
                for b in range(BATCH):
                    if (j, b) == (0, 2):
                        dve.wait_ge(x0_rest_loaded, 16)
                    norm(j, b, False)

            for n in range(2):
                nc.vector.memset(vx[n][:, :, P:SUM], 1.0).then_inc(ones_made, 1)
            block_stats(0)
            for j in range(BLOCKS):
                for part in range(BATCH, 11 + BATCH):
                    if part == 11:
                        after(dve, xn_turned, j)
                    norm(j, part, False)
                if j == 0:
                    for s in reversed(range(MISC)):
                        split_tail(s, MISC - s, early[:, s * PIECE:(s + 1) * PIECE])
                    norm_turn(0, Y[1])
                    block_stats(1)
                else:
                    if j + 1 < BLOCKS:
                        block_stats(j + 1)
                    logits(j - 1, C)
                    norm_turn(j, Y[1])
            for part in range(STEPS):
                route(0, part)
            logits(BLOCKS - 1, C)
            dve.wait_ge(kvsum_done, 1)
            for g in reversed(range(2 * BATCH)):
                b, h, kv = g // 2, g % 2, kvsum[g]
                nc.vector.tensor_tensor(BD[:, b, h, :], mask, kv[:, 0:P], ALU.mult).then_inc(kvsum_masked, 1)
                nc.vector.tensor_tensor(KS[:, b, h, :], mask[:, ::HEAD], kv[:, P:SUM].broadcast_to([P, P // HEAD]),
                                        ALU.mult).then_inc(kvsum_masked, 1)
            dve.wait_ge(pieces_split, EARLY)
            mark(nc.vector.memset(US[:, :, SEQ:SLOTS_T + 8], 0.0))

            def step(tick, i):
                if tick is None:
                    return
                if i % HALF == 0:
                    dve.wait_ge(u_in_ring, 2 * tick + i // HALF + 1)
                dve.wait_ge(state_done, STEPS * tick + i + 1)
                nc.vector.tensor_tensor_scan(zbuf[:, :], gam[:, :], ring[:, i, :], 0.0, ALU.mult, ALU.add)\
                  .then_inc(z_done, 1)

            def gated(n, a):
                dve.wait_ge(silu_done, n + 1)
                dve.wait_ge(up_done, n + 1)
                after(dve, htail_done, n - 1)
                nc.vector.tensor_tensor(h32[a], sg[a], U[a][:, :], ALU.mult).then_inc(gated_done, 1)

            def routed(phase, last, n, a):
                dve.wait_ge(gated_done, n + 1)
                dve.wait_ge(spread_copied, spreads(phase, last))
                nc.vector.tensor_tensor(h32[a], h32[a], spread_slot(phase, last), ALU.mult).then_inc(h_done, 1)

            for phase, (layer, j) in enumerate(PHASES):
                def pair(k, tick, pieces, woven):
                    def step_and(i):
                        step(tick, i)
                        for name, (block_, first) in woven:
                            share[name](block_, first + i)
                    n = chunks_before(layer, j) + 2 * k
                    for a in range(2):
                        step_and(HALF * a)
                        if a or not isinstance(k, int) or k:
                            routed(phase, False, n + a - 1, 1 - a)
                        elif phase:
                            routed(phase - 1, phase > BLOCKS, n - 1, 1)
                        for i in range(1, HALF - 1):
                            step_and(HALF * a + i)
                        gated(n + a, a)
                        step_and(HALF * a + HALF - 1)
                    for a, piece in enumerate(pieces):
                        split_tail(slot_of(piece), piece, stage[:, piece % 2 if len(pieces) == 1 else a, :])
                run_phase(dve, phase, pair, share)
            routed(len(PHASES) - 1, True, chunks_before(*PHASES[-1]) + CHUNKS[1] - 1, 1)
            dve.wait_ge(down_done, chunks_before(*PHASES[-1]) + CHUNKS[1])
            nc.vector.tensor_scalar(yT[1], Y[(len(PHASES) - 1) % 2][1][:, :], Y_DESCALE, out_bias(1, 1),
                                    ALU.mult, ALU.add)\
              .then_inc(y_copied, 1)
            sum_turn(len(PHASES) - 1, Y[(len(PHASES) - 1) % 2])

        @block.gpsimd
        def _(pool):
            nc.gpsimd.memset(zeros[:, :], 0.0).then_inc(zeros_made, 1)

            def split_tail(s, heads, n):
                scaled = early[:, s * PIECE:(s + 1) * PIECE]
                pool.wait_ge(heads_split, heads + 1)
                nc.gpsimd.tensor_scalar(scaled, scaled, W_SCALE, None, ALU.mult).then_inc(early_scaled, 1)
                pool.wait_ge(early_scaled, n + 1)
                if n == 1:
                    pool.wait_ge(pieces_split, CHUNK0)
                nc.gpsimd.tensor_tensor(W[:, s, 1, :], scaled, W[:, s, 0, :], ALU.subtract).then_inc(pieces_split, 1)

            split_tail(MISC, 0, 0)
            nc.gpsimd.memset(gam[:, :], 0.0).then_inc(consts_made, 1)
            pool.wait_ge(consts_loaded, 32)
            pool.wait_ge(consts_made, 1)
            for b in range(BATCH):
                nc.gpsimd.tensor_copy(gam[:, :].rearrange("p (c b two) -> p c b two", b=BATCH, two=2)[:, :, b, 1],
                                      vec[:, 0:KH]).then_inc(consts_made, 1)
            nc.gpsimd.tensor_tensor(ubias[:, :], vec[:, KH:2 * KH], vec[:, 2 * KH:3 * KH], ALU.add)\
              .then_inc(consts_made, 1)
            nc.gpsimd.tensor_copy(identb[:, :], ident).then_inc(consts_made, 1)
            nc.gpsimd.memset(h_scale[:, :, :], H_SCALE).then_inc(pool_order, 1)
            nc.gpsimd.memset(sel[:, :, :], 0.0).then_inc(pool_order, 1)
            pool.wait_ge(pool_order, 2)
            for r, at in enumerate(SPLIT_AT):
                nc.gpsimd.memset(sel[at:at + E0, :, :], 1.0).then_inc(pool_order, 1)
                pool.wait_ge(pool_order, 3 + r)
                for n, units in enumerate((UNITS0, UNITS1, UNITS_LAST)):
                    rows = sel[at:at + E0, n, :]
                    done = 2 * (3 * r + n)
                    after(pool, sel_made, done)
                    nc.gpsimd.affine_select(out=rows, in_=rows, compare_op=ALU.is_ge, fill=0.0, base=0,
                                            pattern=[[1, P]], channel_multiplier=-units).then_inc(sel_made, 1)
                    pool.wait_ge(sel_made, done + 1)
                    nc.gpsimd.affine_select(out=rows, in_=rows, compare_op=ALU.is_ge, fill=0.0, base=units - 1,
                                            pattern=[[-1, P]], channel_multiplier=units).then_inc(sel_made, 1)
            pool.wait_ge(sel_made, 2 * 3 * len(SPLIT_AT))
            for n, s in enumerate(range(CHUNK0, EARLY)):
                split_tail(s, s, n + 1)

            def h_tail(n, a):
                pool.wait_ge(hhead_done, n + 1)
                nc.gpsimd.tensor_tensor(hl[:, a, :], h32[a], hh[:, a, :], ALU.subtract).then_inc(htail_done, 1)

            def rows_of(half, which):
                return ring[:, half * HALF:(half + 1) * HALF, which::2].rearrange("p r l -> p l r")

            def take_u(tick, half):
                nc.gpsimd.tensor_copy(rows_of(half, 1), US[:, :, DS(STEPS * tick + half * HALF, HALF)])\
                  .then_inc(u_in_ring, 1)

            def keep_states(tick, half):
                span = US16[:, :, DS(STEPS * tick + half * HALF, HALF), :]
                kept = state_scaled[:, half, :, :]
                nc.gpsimd.tensor_tensor(kept, rows_of(half, 0), h_scale[:, :, :], ALU.mult)\
                  .then_inc(state_scaled_done, 1)
                pool.wait_ge(state_scaled_done, 2 * tick + half + 1)
                nc.gpsimd.tensor_copy(span[:, :, :, 0], kept).then_inc(state_head, 1)
                pool.wait_ge(state_head, 2 * tick + half + 1)
                nc.gpsimd.tensor_tensor(span[:, :, :, 1], kept, span[:, :, :, 0], ALU.subtract)\
                  .then_inc(states_out, 1)

            def first_tick():
                pool.wait_ge(u_copied, KH)
                take_u(0, 0)

            def more_inputs(blocks):
                pool.wait_ge(u_copied, KH * blocks)

            share = {"first_tick": first_tick, "more_inputs": more_inputs}

            for phase, (layer, j) in enumerate(PHASES):
                def pair(k, tick, pieces, woven):
                    n = chunks_before(layer, j) + 2 * k
                    if tick is not None:
                        pool.wait_ge(state_done, STEPS * tick + 1)
                        if not isinstance(tick, int) or tick:
                            keep_states(tick - 1, 1)
                        take_u(tick, 1)
                    if phase or not isinstance(k, int) or k:
                        h_tail(n - 1, 1)
                    if tick is not None:
                        pool.wait_ge(state_done, STEPS * tick + HALF + 1)
                        keep_states(tick, 0)
                        take_u(tick + 1, 0)
                    h_tail(n, 0)
                run_phase(pool, phase, pair, share)
            h_tail(chunks_before(*PHASES[-1]) + CHUNKS[1] - 1, 1)


def kernel(**inputs):
    import numpy as np
    import concourse.bacc as bacc
    from concourse.bass_utils import run_bass_kernel_spmd

    a = {n: np.asarray(v) for n, v in inputs.items()}

    def over_rows(m):
        t = np.ascontiguousarray(m.T)
        return t.reshape(t.shape[0] // P, P, t.shape[1])

    def chunk_rows(parts, chunks, last):
        rows = np.full((chunks, P), -1)
        at, at_last = 0, 0
        for first, count, units in parts:
            full = chunks - last
            rows[:full, at:at + units] = first + np.arange(full * units).reshape(full, units)
            at += units
            rest = count - full * units
            if rest:
                rows[full, at_last:at_last + rest] = first + full * units + np.arange(rest)
                at_last += rest
        return rows

    def chunk_pieces(gates, ups, downs, rows):
        res = np.zeros((len(rows), P, PIECE), gates.dtype)
        for c, units in enumerate(rows):
            gate, up, down = (np.where(units[:, None] < 0, m.dtype.type(0), m[units]) for m in (gates, ups, downs))
            for i, m in enumerate((gate, up)):
                t = over_rows(m)
                for kd in range(KD):
                    res[c, :, (i * KD + kd) * P:(i * KD + kd + 1) * P] = t[kd]
            res[c, :, 2 * KD * P:] = down
        return res

    def rows_of_down(w):
        return np.swapaxes(w, 1, 2).reshape(-1, DIM)

    qkv = over_rows(a["L0_attn_w_qkv"])
    proj = over_rows(a["L0_attn_w_proj"])
    gate0, gate1 = over_rows(a["L0_ffn_gate_w"]), over_rows(a["L1_ffn_gate_weight"])
    w_in, w_out = over_rows(a["L1_attn_W_in"]), over_rows(a["L1_attn_W_out"])
    misc = np.zeros((P, PIECE), qkv.dtype)
    body = np.concatenate([proj[0], proj[1], gate0[0], gate0[1], gate1[0], gate1[1]], axis=1)
    misc[:, :body.shape[1]] = body
    last = np.zeros((P, PIECE), qkv.dtype)
    last[:, :2 * DIM] = np.concatenate([w_out[2], w_out[3]], axis=1)
    rows0 = chunk_rows([(e * FE, FE, UNITS0) for e in range(E0)], CH0, 0)
    rows1 = chunk_rows([(e * FE, FE, UNITS1) for e in range(E1)] + [(E1 * FE, SHARED * FE, UNITS_SHARED)], CH1, 1)
    moe0 = chunk_pieces(a["L0_ffn_w_gate"].reshape(-1, DIM), a["L0_ffn_w_up"].reshape(-1, DIM),
                        rows_of_down(a["L0_ffn_w_down"]), rows0)
    moe1 = chunk_pieces(np.concatenate([a["L1_ffn_w_gate"].reshape(-1, DIM), a["L1_ffn_sw_gate"]]),
                        np.concatenate([a["L1_ffn_w_up"].reshape(-1, DIM), a["L1_ffn_sw_up"]]),
                        np.concatenate([rows_of_down(a["L1_ffn_w_down"]), a["L1_ffn_sw_down"].T]), rows1)
    rec = [np.concatenate([w_in[0], w_out[0]], axis=1), np.concatenate([w_in[1], w_out[1]], axis=1), last]
    weights = np.ascontiguousarray(np.concatenate([np.stack([qkv[0], qkv[1], misc]), moe0, np.stack(rec), moe1]))

    def column(v):
        return v.reshape(-1, P).T

    vectors = np.ascontiguousarray(np.concatenate([column(a[n]) for n in (
        "L1_attn_gamma", "L1_attn_beta", "L1_attn_b_in", "L0_attn_b_proj", "L1_attn_b_out")], axis=1))
    consts = np.concatenate([np.eye(P), np.kron(np.eye(P // HEAD), np.ones((HEAD, HEAD)))], axis=1).astype(np.float32)
    x = np.ascontiguousarray(a["L0_attn_x"])

    nc = bacc.Bacc("TRN2", target_bir_lowering=False, num_devices=1)
    f32 = mybir.dt.float32
    arrays = {"x": x, "weights": weights, "consts": consts, "vectors": vectors}
    aps = [nc.dram_tensor(n, v.shape, f32, kind="ExternalInput").ap() for n, v in arrays.items()]
    out = nc.dram_tensor("out", x.shape, f32, kind="ExternalOutput").ap()
    build(nc, *aps, out)
    r = run_bass_kernel_spmd(nc, [arrays], core_ids=[0])
    return r.results[0]["out"]
```
